# Optimizing a Trainium2 kernel written in Bass

```python
import numpy as np
import jax
import jax.numpy as jnp

def _softmax(x, axis=-1):
    return jax.nn.softmax(x, axis=axis)

def _gelu(x):
    return jax.nn.gelu(x, approximate=True)

def _silu(x):
    return jax.nn.silu(x)

def _sigmoid(x):
    return jax.nn.sigmoid(x)

def _layernorm(x, axis=-1, eps=1e-05):
    m = jnp.mean(x, axis=axis, keepdims=True)
    v = jnp.var(x, axis=axis, keepdims=True)
    return (x - m) / jnp.sqrt(v + eps)

def _scatter_add(tgt, idx, src, axis=0):
    return tgt.at[idx].add(src)

def _segment_sum(src, seg, n):
    return jax.ops.segment_sum(src, seg, n)
kernel_name = 'mk_gps_d1_gnn_r8_bbda6b'

def setup_inputs(seed: int=0):
    np.random.seed(seed)
    _w = jnp.asarray

    def _rec_inputs():
        import jax
        import jax.numpy as jnp
        _gk = jax.random.key(seed)
        x = -0.0002117 + 1 * jax.random.normal(jax.random.fold_in(_gk, 1), (6250, 256), jnp.float32)
        src = jax.random.randint(jax.random.fold_in(_gk, 2), (100000,), 0, 6250, jnp.int32)
        dst = jnp.minimum((6250 * jax.random.uniform(jax.random.fold_in(_gk, 3), (100000,)) ** 2.0).astype(jnp.int32), 49999)
        _o = jnp.argsort(dst, stable=True)
        src = src[_o]
        dst = dst[_o]
        edge_attr_256 = -5.16925e-05 + 1.00005 * jax.random.normal(jax.random.fold_in(_gk, 12), (100000, 256), jnp.float32)
        return (x, src, dst, edge_attr_256)
    x, src, dst, edge_attr_256 = _rec_inputs()

    def _L0_gnn_setup():
        import jax, jax.numpy as jnp
        import numpy as np
        N_NODES = 12500
        N_EDGES = 50000
        C = 256
        NUM_GRAPHS = 512
        EPS = 1e-05
        key = jax.random.key(seed)
        ks = jax.random.split(key, 12)
        x = jax.random.normal(ks[0], (N_NODES, C), dtype=jnp.float32)
        edge_index = jax.random.randint(ks[1], (2, N_EDGES), 0, N_NODES, dtype=jnp.int32)
        edge_attr = jax.random.normal(ks[2], (N_EDGES, C), dtype=jnp.float32)
        batch = jnp.sort(jax.random.randint(ks[3], (N_NODES,), 0, NUM_GRAPHS, dtype=jnp.int32))
        s1 = 1.0 / np.sqrt(C)
        s2 = 1.0 / np.sqrt(2 * C)
        W1 = jax.random.normal(ks[4], (C, 2 * C), dtype=jnp.float32) * s1
        b1 = jnp.zeros((2 * C,), dtype=jnp.float32)
        bn_gamma = jnp.ones((2 * C,), dtype=jnp.float32)
        bn_beta = jnp.zeros((2 * C,), dtype=jnp.float32)
        W2 = jax.random.normal(ks[5], (2 * C, C), dtype=jnp.float32) * s2
        b2 = jnp.zeros((C,), dtype=jnp.float32)
        ln_w = jnp.ones((C,), dtype=jnp.float32)
        ln_b = jnp.zeros((C,), dtype=jnp.float32)
        gn_w = jnp.ones((C,), dtype=jnp.float32)
        gn_b = jnp.zeros((C,), dtype=jnp.float32)
        gn_ms = jnp.ones((C,), dtype=jnp.float32)
        return dict(x=x, edge_index=edge_index, edge_attr=edge_attr, batch=batch, W1=W1, b1=b1, bn_gamma=bn_gamma, bn_beta=bn_beta, W2=W2, b2=b2, ln_w=ln_w, ln_b=ln_b, gn_w=gn_w, gn_b=gn_b, gn_ms=gn_ms)
    _L0_gnn_all = _L0_gnn_setup()
    _L0_gnn_in = {k: v for k, v in _L0_gnn_all.items() if k in ('W1', 'b1', 'bn_gamma', 'bn_beta', 'W2', 'b2', 'ln_w', 'ln_b', 'gn_w', 'gn_b', 'gn_ms')}
    del _L0_gnn_all

    def _L0_mix_setup():
        import jax, jax.numpy as jnp
        import numpy as np
        import math
        EMBED = 256
        HEADS = 4
        HEAD_DIM = EMBED // HEADS
        OUT_DIM = 256
        LN_EPS = 1e-05

        def _qkv_init(key):
            spread = math.sqrt(3.0 / EMBED)
            gain, delta = (0.01, 0.01)
            w = jax.random.uniform(key, (EMBED, EMBED), minval=-spread, maxval=spread) * gain
            return w + delta * jnp.eye(EMBED, dtype=w.dtype)

        def _layer_norm(x, g, b):
            mu = jnp.mean(x, axis=-1, keepdims=True)
            var = jnp.mean(jnp.square(x - mu), axis=-1, keepdims=True)
            return (x - mu) * jax.lax.rsqrt(var + LN_EPS) * g + b

        def _split_heads(x, B, S):
            return x.reshape(B, S, HEADS, HEAD_DIM).transpose(0, 2, 1, 3)
        key = jax.random.key(seed)
        ks = jax.random.split(key, 6)
        seq = jax.random.normal(ks[0], (4, 1024, EMBED), dtype=jnp.float32)
        wq = _qkv_init(ks[1])
        wk = _qkv_init(ks[2])
        wv = _qkv_init(ks[3])
        bound = 1.0 / math.sqrt(EMBED)
        wo = jax.random.uniform(ks[4], (OUT_DIM, EMBED), minval=-bound, maxval=bound)
        bo = jax.random.uniform(ks[5], (OUT_DIM,), minval=-bound, maxval=bound)
        ln_k_g = jnp.ones((HEAD_DIM,), jnp.float32)
        ln_k_b = jnp.zeros((HEAD_DIM,), jnp.float32)
        ln_v_g = jnp.ones((HEAD_DIM,), jnp.float32)
        ln_v_b = jnp.zeros((HEAD_DIM,), jnp.float32)
        return {'seq': seq, 'wq': wq, 'wk': wk, 'wv': wv, 'wo': wo, 'bo': bo, 'ln_k_g': ln_k_g, 'ln_k_b': ln_k_b, 'ln_v_g': ln_v_g, 'ln_v_b': ln_v_b}
    _L0_mix_all = _L0_mix_setup()
    _L0_mix_in = {k: v for k, v in _L0_mix_all.items() if k in ('wq', 'wk', 'wv', 'wo', 'bo', 'ln_k_g', 'ln_k_b', 'ln_v_g', 'ln_v_b')}
    del _L0_mix_all

    def _L0_ffn_setup():
        import jax, jax.numpy as jnp
        import numpy as np
        NUM_EXPERTS = 8
        TOP_K = 2
        B, S, D = (8, 1024, 256)

        def _moe(tokens, router_w, w1, b1, w2, b2):
            N = tokens.shape[0]
            E = router_w.shape[0]
            logits = tokens.astype(jnp.float32) @ router_w.astype(jnp.float32).T
            probs = jax.nn.softmax(logits, axis=-1)
            rw, re = jax.lax.top_k(probs, TOP_K)
            if TOP_K > 1:
                rw = rw / jnp.maximum(rw.sum(-1, keepdims=True), 1e-12)
            rw = rw.astype(tokens.dtype)
            combine = jnp.zeros((N, E), tokens.dtype).at[jnp.arange(N)[:, None], re].set(rw)
            out = tokens
            for e in range(E):
                h = jax.nn.gelu(tokens @ w1[e] + b1[e], approximate=False)
                y = h @ w2[e] + b2[e]
                out = out + combine[:, e:e + 1] * y
            return out
        key = jax.random.key(seed)
        ks = jax.random.split(key, 4)
        scale = 1.0 / np.sqrt(D).astype(np.float32)
        return {'input_embeddings': jax.random.normal(ks[0], (B, S, D), jnp.float32), 'router_w': jax.random.normal(ks[1], (NUM_EXPERTS, D), jnp.float32) * scale, 'w1': jax.random.normal(ks[2], (NUM_EXPERTS, D, D), jnp.float32) * scale, 'b1': jnp.zeros((NUM_EXPERTS, D), jnp.float32), 'w2': jax.random.normal(ks[3], (NUM_EXPERTS, D, D), jnp.float32) * scale, 'b2': jnp.zeros((NUM_EXPERTS, D), jnp.float32)}
    _L0_ffn_all = _L0_ffn_setup()
    _L0_ffn_in = {k: v for k, v in _L0_ffn_all.items() if k in ('router_w', 'w1', 'b1', 'w2', 'b2')}
    del _L0_ffn_all
    return {'x': x, 'src': src, 'dst': dst, 'edge_attr_256': edge_attr_256, 'L0_gnn_W1': _L0_gnn_in['W1'], 'L0_gnn_b1': _L0_gnn_in['b1'], 'L0_gnn_bn_gamma': _L0_gnn_in['bn_gamma'], 'L0_gnn_bn_beta': _L0_gnn_in['bn_beta'], 'L0_gnn_W2': _L0_gnn_in['W2'], 'L0_gnn_b2': _L0_gnn_in['b2'], 'L0_gnn_ln_w': _L0_gnn_in['ln_w'], 'L0_gnn_ln_b': _L0_gnn_in['ln_b'], 'L0_gnn_gn_w': _L0_gnn_in['gn_w'], 'L0_gnn_gn_b': _L0_gnn_in['gn_b'], 'L0_gnn_gn_ms': _L0_gnn_in['gn_ms'], 'L0_mix_wq': _L0_mix_in['wq'], 'L0_mix_wk': _L0_mix_in['wk'], 'L0_mix_wv': _L0_mix_in['wv'], 'L0_mix_wo': _L0_mix_in['wo'], 'L0_mix_bo': _L0_mix_in['bo'], 'L0_mix_ln_k_g': _L0_mix_in['ln_k_g'], 'L0_mix_ln_k_b': _L0_mix_in['ln_k_b'], 'L0_mix_ln_v_g': _L0_mix_in['ln_v_g'], 'L0_mix_ln_v_b': _L0_mix_in['ln_v_b'], 'L0_ffn_router_w': _L0_ffn_in['router_w'], 'L0_ffn_w1': _L0_ffn_in['w1'], 'L0_ffn_b1': _L0_ffn_in['b1'], 'L0_ffn_w2': _L0_ffn_in['w2'], 'L0_ffn_b2': _L0_ffn_in['b2']}

def reference(x, src, dst, edge_attr_256, L0_gnn_W1, L0_gnn_b1, L0_gnn_bn_gamma, L0_gnn_bn_beta, L0_gnn_W2, L0_gnn_b2, L0_gnn_ln_w, L0_gnn_ln_b, L0_gnn_gn_w, L0_gnn_gn_b, L0_gnn_gn_ms, L0_mix_wq, L0_mix_wk, L0_mix_wv, L0_mix_wo, L0_mix_bo, L0_mix_ln_k_g, L0_mix_ln_k_b, L0_mix_ln_v_g, L0_mix_ln_v_b, L0_ffn_router_w, L0_ffn_w1, L0_ffn_b1, L0_ffn_w2, L0_ffn_b2):
    import jax
    import jax.numpy as jnp

    def _L0_gnn_ref(x, edge_index, edge_attr, batch, W1, b1, bn_gamma, bn_beta, W2, b2, ln_w, ln_b, gn_w, gn_b, gn_ms):
        import jax, jax.numpy as jnp
        import numpy as np
        N_NODES = 12500
        N_EDGES = 50000
        C = 256
        NUM_GRAPHS = 512
        EPS = 1e-05
        src, dst = (edge_index[0], edge_index[1])
        msg = jax.nn.relu(x[src] + edge_attr)
        agg = jnp.zeros_like(x).at[dst].add(msg)
        h = x + agg
        h = h @ W1 + b1
        mu = jnp.mean(h, axis=0)
        var = jnp.mean((h - mu) ** 2, axis=0)
        h = (h - mu) / jnp.sqrt(var + EPS) * bn_gamma + bn_beta
        h = jax.nn.relu(h) @ W2 + b2
        cnt = jax.ops.segment_sum(jnp.ones((h.shape[0],), h.dtype), batch, NUM_GRAPHS)
        denom = jnp.maximum(cnt, 1.0) * C
        mean_g = jax.ops.segment_sum(h.sum(axis=1), batch, NUM_GRAPHS) / denom
        h = h - mean_g[batch][:, None]
        var_g = jax.ops.segment_sum((h * h).sum(axis=1), batch, NUM_GRAPHS) / denom
        h = h * jax.lax.rsqrt(var_g + EPS)[batch][:, None] * ln_w + ln_b
        cnt_c = jnp.maximum(cnt, 1.0)[:, None]
        mean = jax.ops.segment_sum(h, batch, NUM_GRAPHS) / cnt_c
        out = h - mean[batch] * gn_ms
        var2 = jax.ops.segment_sum(out * out, batch, NUM_GRAPHS) / cnt_c
        out = out * jax.lax.rsqrt(var2 + EPS)[batch] * gn_w + gn_b
        out = jax.nn.relu(out)
        return x + out

    def _L0_mix_ref(seq, wq, wk, wv, wo, bo, ln_k_g, ln_k_b, ln_v_g, ln_v_b):
        import jax, jax.numpy as jnp
        import numpy as np
        import math
        EMBED = 256
        HEADS = 4
        HEAD_DIM = EMBED // HEADS
        OUT_DIM = 256
        LN_EPS = 1e-05

        def _qkv_init(key):
            spread = math.sqrt(3.0 / EMBED)
            gain, delta = (0.01, 0.01)
            w = jax.random.uniform(key, (EMBED, EMBED), minval=-spread, maxval=spread) * gain
            return w + delta * jnp.eye(EMBED, dtype=w.dtype)

        def _layer_norm(x, g, b):
            mu = jnp.mean(x, axis=-1, keepdims=True)
            var = jnp.mean(jnp.square(x - mu), axis=-1, keepdims=True)
            return (x - mu) * jax.lax.rsqrt(var + LN_EPS) * g + b

        def _split_heads(x, B, S):
            return x.reshape(B, S, HEADS, HEAD_DIM).transpose(0, 2, 1, 3)
        B, S, _ = seq.shape
        q = _split_heads(seq @ wq.T, B, S)
        k = _split_heads(seq @ wk.T, B, S)
        v = _split_heads(seq @ wv.T, B, S)
        k = _layer_norm(k, ln_k_g, ln_k_b)
        v = _layer_norm(v, ln_v_g, ln_v_b)
        kv = jnp.einsum('bhsd,bhse->bhde', k, v) / S
        ga = jnp.einsum('bhsd,bhde->bhse', q, kv)
        ga = ga.transpose(0, 2, 1, 3).reshape(B, S, EMBED)
        return ga @ wo.T + bo

    def _L0_ffn_ref(input_embeddings, router_w, w1, b1, w2, b2):
        import jax, jax.numpy as jnp
        import numpy as np
        NUM_EXPERTS = 8
        TOP_K = 2
        B, S, D = (8, 1024, 256)

        def _moe(tokens, router_w, w1, b1, w2, b2):
            N = tokens.shape[0]
            E = router_w.shape[0]
            logits = tokens.astype(jnp.float32) @ router_w.astype(jnp.float32).T
            probs = jax.nn.softmax(logits, axis=-1)
            rw, re = jax.lax.top_k(probs, TOP_K)
            if TOP_K > 1:
                rw = rw / jnp.maximum(rw.sum(-1, keepdims=True), 1e-12)
            rw = rw.astype(tokens.dtype)
            combine = jnp.zeros((N, E), tokens.dtype).at[jnp.arange(N)[:, None], re].set(rw)
            out = tokens
            for e in range(E):
                h = jax.nn.gelu(tokens @ w1[e] + b1[e], approximate=False)
                y = h @ w2[e] + b2[e]
                out = out + combine[:, e:e + 1] * y
            return out
        b, s, d = input_embeddings.shape
        tokens = input_embeddings.reshape(b * s, d)
        return _moe(tokens, router_w, w1, b1, w2, b2).reshape(b, s, d)
    edge_index = jnp.stack([src, dst])
    batch0 = jnp.zeros((6250,), jnp.int32)
    xn = _layernorm(x, axis=-1)
    x = x + _L0_gnn_ref(xn, edge_index, edge_attr_256, batch0, L0_gnn_W1, L0_gnn_b1, L0_gnn_bn_gamma, L0_gnn_bn_beta, L0_gnn_W2, L0_gnn_b2, L0_gnn_ln_w, L0_gnn_ln_b, L0_gnn_gn_w, L0_gnn_gn_b, L0_gnn_gn_ms) + _L0_mix_ref(xn[None], L0_mix_wq, L0_mix_wk, L0_mix_wv, L0_mix_wo, L0_mix_bo, L0_mix_ln_k_g, L0_mix_ln_k_b, L0_mix_ln_v_g, L0_mix_ln_v_b)[0]
    x = x + _L0_ffn_ref(_layernorm(x, axis=-1)[None], L0_ffn_router_w, L0_ffn_w1, L0_ffn_b1, L0_ffn_w2, L0_ffn_b2)[0]
    return x

_drawn_inputs = setup_inputs


def setup_inputs(seed=0):
    import zlib

    import numpy as np

    out = dict(_drawn_inputs(seed))
    spreads = {'L0_gnn_b1': (0.0, 2.0),
     'L0_gnn_bn_gamma': (1.0, 0.2),
     'L0_gnn_bn_beta': (0.0, 0.353),
     'L0_gnn_b2': (0.0, 0.388),
     'L0_gnn_ln_w': (1.0, 0.6),
     'L0_gnn_ln_b': (0.0, 0.46),
     'L0_gnn_gn_w': (1.0, 0.2),
     'L0_gnn_gn_b': (0.0, 0.291),
     'L0_gnn_gn_ms': (1.0, 0.2),
     'L0_mix_ln_k_g': (1.0, 0.6),
     'L0_mix_ln_k_b': (0.0, 0.8),
     'L0_mix_ln_v_g': (1.0, 0.6),
     'L0_mix_ln_v_b': (0.0, 0.8),
     'L0_ffn_b1': (0.0, 0.498),
     'L0_ffn_b2': (0.0, 0.336)}
    factors = {'L0_mix_wq': 8.0, 'L0_mix_wk': 8.0, 'L0_mix_wv': 8.0, 'L0_mix_wo': 8.0, 'L0_mix_bo': 4.149}
    for name, (base, spread) in spreads.items():
        noise = np.random.default_rng([zlib.crc32(name.encode()), seed]).standard_normal(out[name].shape)
        drawn = base * np.exp(spread * noise) if base else spread * noise
        out[name] = jnp.asarray(drawn.astype(out[name].dtype))
    for name, factor in factors.items():
        out[name] = (out[name] * factor).astype(out[name].dtype)
    return out
```

```python
from contextlib import ExitStack

import concourse.bass as bass
from concourse import mybir

ALU = mybir.AluOpType
ACT = mybir.ActivationFunctionType
AX = mybir.AxisListType
F32 = mybir.dt.float32
F32R = mybir.dt.float32r
I32 = mybir.dt.int32
U32 = mybir.dt.uint32

P = 128
EPS = 1e-5
HEAD = 64
SLOTS = 4
J = 8
WIN = 160
TILES = 4
CH = TILES * P
CREDIT = 1
RSQRT_MAGIC = 0x5F3759DF
RSQRT_STEPS = 11
STATS_STEPS = 4 + RSQRT_STEPS


class Chunk:

    def __init__(self, c, n, i=None, u=None):
        self.c, self.n, self.i, self.u = c, n, i, u
        self.rows, self.tiles = min(n, P), (n + P - 1) // P


class Supertile:

    def __init__(self, s, parts=P, q=None, u=0):
        self.s, self.q, self.u, self.r, self.b = s, q, u, slice(0, parts), u % 2


class Steps:

    def __init__(self, eng, sem, base=0):
        self.eng, self.sem, self.base, self.n = eng, sem, base, 0

    def run(self, ins):
        self.n += 1
        ins.then_inc(self.sem, 1)
        self.eng.wait_ge(self.sem, self.base + self.n)


def rsqrt_steps(dve, steps, v, y, h):
    vi, yi = v.bitcast(I32), y.bitcast(I32)
    steps.run(dve.tensor_scalar(yi, vi, 1, None, ALU.logical_shift_right))
    steps.run(dve.tensor_scalar(yi, yi, -1.0, float(RSQRT_MAGIC), ALU.mult, ALU.add))
    for _ in range(3):
        steps.run(dve.scalar_tensor_tensor(h, y, -0.5, y, ALU.mult, ALU.mult))
        steps.run(dve.tensor_tensor(h, h, v, ALU.mult))
        steps.run(dve.scalar_tensor_tensor(y, h, 1.5, y, ALU.add, ALU.mult))


def stats_steps(dve, steps, st, mean, var, tmp, C, rstd):
    dve.tensor_tensor(mean, st[:, :, 1], st[:, :, 4], ALU.add)
    dve.tensor_tensor(tmp, st[:, :, 1], st[:, :, 4], ALU.subtract)
    steps.run(dve.tensor_tensor(var, st[:, :, 2], st[:, :, 5], ALU.add))
    dve.tensor_scalar(mean, mean, 0.5, None, ALU.mult)
    dve.tensor_scalar(var, var, 1.0 / C, EPS, ALU.mult, ALU.add)
    steps.run(dve.scalar_tensor_tensor(tmp, tmp, 0.25, tmp, ALU.mult, ALU.mult))
    steps.run(dve.tensor_tensor(var, var, tmp, ALU.add))
    rsqrt_steps(dve, steps, var, rstd, tmp)


def build(nc, x, src, dst, edge_attr, gnn, mix, ffn, out):
    N, C = x.shape
    E = edge_attr.shape[0]
    H = gnn["W1"].shape[1]
    NE = ffn["w1"].shape[0]
    KC = C // P
    KH = H // P
    NCH = N // CH
    TAIL = N - NCH * CH
    ST = P * J
    NST = E // ST
    ETAIL = (E - NST * ST) // J
    NBASE = NST + 1
    NCOL = NST + SLOTS - NST % SLOTS
    ROUNDS = NST // SLOTS
    NWIN = (N + WIN - 1) // WIN
    AGG = max(NWIN * WIN, N + WIN)
    NH = C // HEAD
    assert TAIL <= P and NST * ST + ETAIL * J == E and ROUNDS == 2 * NCH and NCH % 2 == 0
    assert NCOL > NST + 1

    xn_dram = nc.dram_tensor("xn_rows", [N, C], F32).ap()
    base_dram = nc.dram_tensor("base_rows", [N, C], F32).ap()

    ctx = ExitStack()
    with ctx:
        ctx.enter_context(nc.allow_non_contiguous_dma(reason="small vectors and tables"))

        def sb(name, shape, dt=F32):
            return ctx.enter_context(nc.sbuf_tensor(name, shape, dt))

        def sem(name):
            return ctx.enter_context(nc.semaphore(name))

        hT = sb("hT", [P, KC, AGG])
        ring = sb("ring", [P, SLOTS * J * C])
        kvraw = sb("kvraw", [P, TILES * 2 * C])
        wkvT = sb("wkvT", [P, KC, 2 * C])
        xc = sb("xc", [P, KC, CH])
        sq = sb("sq", [P, 2 * C])
        wq = sb("wq", [P, KC, C])
        woT = sb("woT", [P, KC, C])
        ident = sb("ident", [P, P])
        ones = sb("ones", [P, P])
        centre = kvraw[:, 0:P]
        amat = wkvT[:, 1, 0:KC * P].rearrange("p (k c) -> p k c", k=KC)
        vrow = sb("vrow", [P, 2, P])
        bo_row = sb("bo_row", [P, C])
        iota = sb("iota", [P, WIN])
        basebc = sb("basebc", [P, NCOL])
        bases = sb("bases", [1, NCOL], I32)
        flag = sb("flag", [1, 2], I32)
        vec = sb("vec", [P, 80])
        st = sb("st", [P, 2, TILES, 6])
        tiny = sb("tiny", [P, 16, TILES])
        rs = sb("rs", [P, 3, TILES * 2 * NH])
        until_ffn = ctx.enter_context(ExitStack())
        big = until_ffn.enter_context(nc.sbuf_tensor("big", [P, KH * N], F32))
        ps = ctx.enter_context(nc.psum_tensor("ps", [P, 8, CH], F32))

        xnT = big[:, 0:KC * N].rearrange("p (k n) -> p k n", k=KC)
        o = KC * N
        e_ring = big[:, o:o + SLOTS * J * C].rearrange("p (s j c) -> p s j c", s=SLOTS, j=J)
        o += SLOTS * J * C
        hot = big[:, o:o + 2 * J * WIN].rearrange("p (s j w) -> p s j w", s=2, j=J)
        o += 2 * J * WIN
        srcT = big[:, o:o + NCOL * J].bitcast(U32)
        o += NCOL * J
        rel = big[:, o:o + NCOL * J]
        o += NCOL * J
        cur = big[:, o:o + SLOTS * J].bitcast(U32).rearrange("p (s j) -> p s j", s=SLOTS)
        o += SLOTS * J
        assert o <= KH * N
        g_ring = ring[:, :].rearrange("p (s j c) -> p s j c", s=SLOTS, j=J)

        CR = TILES * C
        rows_in = [ring[:, s * CR:(s + 1) * CR].rearrange("p (t c) -> p t c", t=TILES) for s in range(2)]
        rows_xn = [ring[:, (2 + s) * CR:(3 + s) * CR].rearrange("p (t c) -> p t c", t=TILES) for s in range(2)]
        ea = big[:, KC * N:KC * N + SLOTS * J * C]
        idx_i = [ea[0:NBASE, k * ST:(k + 1) * ST].bitcast(I32) for k in range(2)]
        idx_f = [ea[0:NBASE, (2 + k) * ST:(3 + k) * ST] for k in range(2)]
        wk_in = ea[:, 4 * ST:4 * ST + KC * C].rearrange("p (k c) -> p k c", k=KC)
        wv_in = ea[:, 4 * ST + KC * C:4 * ST + 2 * KC * C].rearrange("p (k c) -> p k c", k=KC)
        wo_in = ea[:, 4 * ST + 2 * KC * C:4 * ST + 3 * KC * C].rearrange("p (k c) -> p k c", k=KC)
        rw_in = ea[0:NE, 4 * ST + 3 * KC * C:4 * ST + 3 * KC * C + C]

        base_row = kvraw[0:1, 2 * P:2 * P + NBASE]

        at = [0]

        def cols(n):
            at[0] += n
            assert at[0] <= 80
            return vec[:, at[0] - n:at[0]]

        v_b1, v_gamma, v_beta = cols(KH), cols(KH), cols(KH)
        v_b2, v_lnw, v_lnb, v_gnw, v_gnb, v_gnms = (cols(KC) for _ in range(6))
        v_kg, v_kb = cols(1), cols(1)
        v_eb1 = cols(NE * KC).rearrange("p (e k) -> p e k", e=NE)
        v_rw = cols(KC * NE).rearrange("p (k e) -> p k e", k=KC)
        s = {name: sem(name) for name in """vectors_in tables_in weights_in rows_in0 rows_in1 rows_done rows_out0 rows_out1 stored0 stored1
                turned0 turned1 copied0 copied1 dve_steps const_pool const_done table_f table_t table_done
                weight_t weight_done hT_in carrier flag_in flag_t flag_c
                e_in0 e_in1 e_in2 e_in3 gathered0 gathered1 gathered2 gathered3 cur0 cur1 cur2 cur3
                summed0 summed1 summed2 summed3 relu0 relu1 relu2 relu3 used0 used1 used2 used3
                windowed0 windowed1 windowed2 windowed3 hot_ready kv_steps
                xc_ready proj_done raw_done sq_done ssq_done scaled kv_done am_steps am_ready r_done r_copied m_done m_copied
                mixed x_in base_added base_out proj_sent kv_zero base_f base_t flag_f flag_steps raw_done1""".split()}
        VECTORS = 16 * (9 + 4 + 2 + 4)
        two = lambda name: [s[f"{name}{k}"] for k in range(2)]
        four = lambda name: [s[f"{name}{k}"] for k in range(SLOTS)]

        def chunk(a, c, n=CH):
            if n == CH:
                return a[bass.ds(c * CH, CH), :].rearrange("(t p) c -> p t c", p=P)
            return a[NCH * CH:N, :].rearrange("(t p) c -> p t c", t=1)

        def chunk_of(i, u):
            return Chunk(2 * i + u, CH, i, u)

        last_chunk = Chunk(NCH, TAIL, NCH // 2, 0)

        def all_chunks(eng, body):
            with eng.Fori(0, NCH // 2) as i:
                for u in range(2):
                    body(chunk_of(i, u))
            body(last_chunk)

        with nc.Block() as block:
            @block.sync
            def _(sp):
                def store(k):
                    sp.wait_ge(s["rows_done"], k.c + 1)
                    sp.dma_start(chunk(xn_dram, k.c, k.n), rows_xn[k.u][0:k.rows, 0:k.tiles, :]).then_inc(two("rows_out")[k.u], 16)

                def stored(k):
                    sp.wait_ge(two("rows_out")[k.u], 16 * (k.i + 1))
                    sp.sem_inc(two("stored")[k.u], 1)

                for u in range(2):
                    sp.dma_start(rows_in[u], chunk(x, u)).then_inc(two("rows_in")[u], 16)
                for idx_in, a in zip(idx_i, (src, dst)):
                    sp.wait_ge(s["const_pool"], 3)
                    sp.dma_start(idx_in[0:NST, :], a[0:NST * ST].rearrange("(s e) -> s e", s=NST)).then_inc(s["tables_in"], 16)
                    sp.dma_start(idx_in[NST:NBASE, 0:ETAIL * J], a[NST * ST:E].rearrange("(s e) -> s e", s=1)).then_inc(s["tables_in"], 16)
                sp.dma_start(bases[0:1, 0:NBASE], bass.AP(dst.tensor, 0, [[1, 1], [ST, NBASE]])).then_inc(s["flag_in"], 16)
                for w_in, w in ((wk_in, mix["wk"]), (wv_in, mix["wv"]), (wo_in, mix["wo"]), (wq, mix["wq"])):
                    sp.dma_start(w_in[:, :, :], w.rearrange("(k p) c -> p k c", p=P)).then_inc(s["weights_in"], 16)
                sp.dma_start(rw_in, ffn["router_w"]).then_inc(s["weights_in"], 16)
                with sp.Fori(0, NCH // 2 - 1) as i:
                    for u in range(2):
                        k = chunk_of(i, u)
                        store(k)
                        sp.dma_start(rows_in[u], chunk(x, 2 * i + u + 2)).then_inc(two("rows_in")[u], 16)
                        stored(k)
                k = chunk_of(NCH // 2 - 1, 0)
                store(k)
                sp.dma_start(rows_in[0][0:TAIL, 0:1, :], chunk(x, NCH, TAIL)).then_inc(s["rows_in0"], 16)
                stored(k)
                store(chunk_of(NCH // 2 - 1, 1))
                store(last_chunk)
                sp.wait_ge(s["copied0"], CREDIT + NCH // 2 + 1)
                sp.wait_ge(s["copied1"], CREDIT + NCH // 2)
                sp.dma_start(hT[:, :, 0:N], xnT).then_inc(s["hT_in"], 16)
                sp.wait_ge(s["hT_in"], 16)
                sp.wait_ge(s["rows_out0"], 16 * (NCH // 2 + 1))
                sp.wait_ge(s["rows_out1"], 16 * (NCH // 2))

            @block.scalar
            def _(act):
                for v, a in ((v_b1, gnn["b1"]), (v_gamma, gnn["bn_gamma"]), (v_beta, gnn["bn_beta"]), (v_b2, gnn["b2"]),
                             (v_lnw, gnn["ln_w"]), (v_lnb, gnn["ln_b"]), (v_gnw, gnn["gn_w"]), (v_gnb, gnn["gn_b"]),
                             (v_gnms, gnn["gn_ms"])):
                    act.dma_start(v, a.rearrange("(k p) -> p k", p=P)).then_inc(s["vectors_in"], 16)
                for half in range(P // HEAD):
                    for v, a in ((v_kg, mix["ln_k_g"]), (v_kb, mix["ln_k_b"])):
                        act.dma_start(v[half * HEAD:(half + 1) * HEAD, :], a.rearrange("(d o) -> d o", o=1)).then_inc(s["vectors_in"], 16)
                act.dma_start(v_eb1, ffn["b1"].rearrange("e (k p) -> p e k", p=P)).then_inc(s["vectors_in"], 16)
                act.dma_start(bo_row[:, :], mix["bo"].partition_broadcast(P)).then_inc(s["vectors_in"], 16)
                for n, a in enumerate((mix["ln_v_g"], mix["ln_v_b"])):
                    for half in range(P // HEAD):
                        act.dma_start(vrow[:, n, half * HEAD:(half + 1) * HEAD], a.partition_broadcast(P)).then_inc(s["vectors_in"], 16)

                act.wait_ge(s["weight_t"], 1)
                for ki in range(KC):
                    ins = act.activation(wkvT[:, ki, :], ps[:, 4 + ki, :], ACT.Copy)
                ins.then_inc(s["weight_done"], 1)
                act.wait_ge(s["weight_t"], 2)
                act.activation(woT[:, :, :], ps[:, 6, :].rearrange("p (k c) -> p k c", k=KC), ACT.Copy)
                act.activation(v_rw, ps[:, 7, 0:KC * NE].rearrange("p (k e) -> p k e", k=KC), ACT.Copy).then_inc(s["weight_done"], 1)

                def copy_turned(k):
                    act.wait_ge(two("turned")[k.u], CREDIT + k.i + 1)
                    act.sem_inc(s["carrier"], 1)
                    for kc in range(KC):
                        ins = act.activation(xnT[:, kc, bass.ds(k.c * CH, k.n)], ps[:, 2 * k.u + kc, 0:k.n], ACT.Copy)
                    ins.then_inc(two("copied")[k.u], 1)

                all_chunks(act, copy_turned)

            @block.vector
            def _(dve):
                dve.memset(ones[:, :], 1.0)
                dve.memset(hT[:, :, N:AGG], 0.0).then_inc(s["const_done"], 1)
                steps = Steps(dve, s["dve_steps"])
                dve.wait_ge(s["const_pool"], 3)
                steps.run(dve.memset(centre[:, :], 0.0))
                for half in range(P // HEAD):
                    d = slice(half * HEAD, (half + 1) * HEAD)
                    dve.memset(centre[d, d], -1.0 / HEAD)
                steps.run(dve.memset(tiny[:, 0, :], 0.0))
                dve.tensor_tensor(centre[:, :], centre[:, :], ident[:, :], ALU.add).then_inc(s["const_done"], 1)

                dve.wait_ge(s["tables_in"], 64)
                dve.tensor_copy(idx_f[0], idx_i[0])
                steps.run(dve.tensor_copy(idx_f[1], idx_i[1]))
                steps.run(dve.tensor_scalar(tiny[0:NBASE, 1, 0:1], idx_f[1][:, 0:1], 1.0, None, ALU.mult))
                dve.tensor_scalar(idx_f[1], idx_f[1], tiny[0:NBASE, 1, 0:1], None, ALU.subtract).then_inc(s["table_f"], 1)
                srcT_v = srcT.rearrange("p (s j) -> p j s", j=J)
                rel_v = rel.rearrange("p (s j) -> p j s", j=J)
                dve.memset(rel, -1.0)
                steps.run(dve.memset(srcT.bitcast(I32), 0))
                for k, table in enumerate((srcT_v, rel_v)):
                    for h in range(2):
                        dve.wait_ge(s["table_t"], 2 * k + h + 1)
                        part = ps[:, 4 + h, 0:J // 2 * NBASE].rearrange("p (j s) -> p j s", j=J // 2)
                        dve.tensor_copy(table[:, h * J // 2:(h + 1) * J // 2, 0:NBASE], part).then_inc(s["table_done"], 1)
                dve.wait_ge(s["flag_in"], 16)
                dve.tensor_copy(base_row, bases[0:1, 0:NBASE]).then_inc(s["base_f"], 1)
                dve.wait_ge(s["base_t"], 1)
                dve.tensor_copy(basebc[:, 0:NBASE], ps[:, 7, 2 * P:2 * P + NBASE])
                n0 = steps.n

                def normalise(k):
                    r, t = slice(0, k.rows), slice(0, k.tiles)
                    xin, xo = rows_in[k.u], rows_xn[k.u]
                    steps = Steps(dve, s["dve_steps"], n0 + k.c * STATS_STEPS)
                    dve.wait_ge(two("rows_in")[k.u], 16 * (k.i + 1))
                    for j in range(k.tiles):
                        ins = dve.bn_stats(st[r, 0, j, :], xin[r, j, :])
                    steps.run(ins)
                    mean, rstd = tiny[r, 2, t], tiny[r, 3, t]
                    stats_steps(dve, steps, st[r, 0, t, :], mean, tiny[r, 4, t], tiny[r, 5, t], C, rstd)
                    assert steps.n == STATS_STEPS
                    dve.wait_ge(two("stored")[k.u], CREDIT + k.i)
                    dve.wait_ge(two("turned")[k.u], CREDIT + k.i)
                    for j in range(k.tiles):
                        ins = dve.tensor_scalar(xo[r, j, :], xin[r, j, :], tiny[r, 2, j:j + 1], tiny[r, 3, j:j + 1],
                                                ALU.subtract, ALU.mult)
                    ins.then_inc(s["rows_done"], 1)

                all_chunks(dve, normalise)

            @block.gpsimd
            def _(pool):
                pool.memset(ident[:, :], 0.0).then_inc(s["const_pool"], 1)
                pool.wait_ge(s["const_pool"], 1)
                pool.affine_select(out=ident[:, :], in_=ident[:, :], compare_op=ALU.not_equal, fill=1.0, base=0,
                                   pattern=[[-1, P]], channel_multiplier=1).then_inc(s["const_pool"], 1)
                pool.iota(iota[:, :], [[1, WIN]], base=0, channel_multiplier=0,
                          allow_small_or_imprecise_dtypes=True)
                pool.memset(ea[:, 0:2 * ST], 0.0).then_inc(s["const_pool"], 1)

            @block.tensor
            def _(pe):
                for credited in two("stored") + two("turned") + two("copied"):
                    pe.sem_inc(credited, CREDIT)
                pe.wait_ge(s["const_pool"], 2)
                pe.wait_ge(s["const_done"], 2)
                pe.wait_ge(s["weights_in"], 80)
                for n, w_in in enumerate((wk_in, wv_in)):
                    for ki in range(KC):
                        for ko in range(KC):
                            ins = pe.matmul(ps[:, 4 + ki, n * C + ko * P:n * C + (ko + 1) * P],
                                            w_in[:, ko, ki * P:(ki + 1) * P], centre[:, :], start=True, stop=True)
                ins.then_inc(s["weight_t"], 1)
                for ki in range(KC):
                    for ko in range(KC):
                        pe.transpose(ps[:, 6, ki * C + ko * P:ki * C + (ko + 1) * P],
                                     wo_in[:, ko, ki * P:(ki + 1) * P], ident[:, :])
                for ki in range(KC):
                    ins = pe.transpose(ps[:, 7, ki * NE:(ki + 1) * NE], rw_in[:, ki * P:(ki + 1) * P],
                                       ident[0:NE, 0:NE])
                ins.then_inc(s["weight_t"], 1)

                pe.wait_ge(s["weight_done"], 1)
                pe.wait_ge(s["table_f"], 1)
                for k in range(2):
                    for h in range(2):
                        if k == 1:
                            pe.wait_ge(s["table_done"], h + 1)
                        for jj in range(J // 2):
                            j = h * J // 2 + jj
                            ins = pe.transpose(ps[:, 4 + h, jj * NBASE:(jj + 1) * NBASE],
                                               idx_f[k].rearrange("s (p j) -> s j p", j=J)[:, j, :],
                                               ident[0:NBASE, 0:NBASE])
                        ins.then_inc(s["table_t"], 1)

                pe.wait_ge(s["weight_done"], 2)
                pe.wait_ge(s["base_f"], 1)
                pe.matmul(ps[:, 7, 2 * P:2 * P + NBASE], ones[0:1, :], base_row, start=True, stop=True).then_inc(s["base_t"], 1)

                def turn(k):
                    pe.wait_ge(s["rows_done"], k.c + 1)
                    pe.wait_ge(two("copied")[k.u], CREDIT + k.i)
                    for kc in range(KC):
                        for t in range(k.tiles):
                            ins = pe.transpose(ps[:, 2 * k.u + kc, t * P:t * P + k.rows],
                                               rows_xn[k.u][0:k.rows, t, kc * P:(kc + 1) * P],
                                               ident[0:k.rows, 0:k.rows])
                    ins.then_inc(two("turned")[k.u], 1)

                all_chunks(pe, turn)

        e_in, gathered, cur_ready, summed, messages, used, windowed = map(
            four, ("e_in", "gathered", "cur", "summed", "relu", "used", "windowed"))
        raw_done = [s["raw_done"], s["raw_done1"]]
        group = TILES * 2 * NH
        mixm = wkvT[:, 0, :].rearrange("p (k c) -> p k c", k=KC)
        rmat = sq[:, :].rearrange("p (k c) -> p k c", k=KC)
        xrows = kvraw[:, 0:TILES * C].rearrange("p (t c) -> p t c", t=TILES)

        def supertile(q, u, parts=P):
            return Supertile(SLOTS * q + u, parts, q, u)

        first_tail, last_tail = supertile(ROUNDS, 0), supertile(ROUNDS, 1, ETAIL)

        def other(k):
            return (k.u - 2, k.q + 1) if k.u >= 2 else (k.u + 2, k.q)

        def node_chunk(c, n=CH):
            return Chunk(c, n)

        tail = node_chunk(NCH, TAIL)

        with nc.Block() as block:
            @block.sync
            def _(sp):
                def load_edges(k):
                    sp.wait_ge(summed[k.u], CREDIT + k.q)
                    rows = edge_attr[bass.ds(k.s * ST, (k.r.stop) * J), :]
                    sp.dma_start(e_ring[k.r, k.u, :, :], rows.rearrange("(p j) c -> p j c", j=J)).then_inc(e_in[k.u], 16)

                def load_rows(k):
                    sp.dma_start(xrows[0:k.rows, 0:k.tiles, :], chunk(x, k.c, k.n)).then_inc(s["x_in"], 16)

                def store_base(k):
                    sp.wait_ge(s["base_added"], CREDIT + k.c + 1)
                    sp.dma_start(chunk(base_dram, k.c, k.n), xrows[0:k.rows, 0:k.tiles, :]).then_inc(s["base_out"], 16)
                    sp.wait_ge(s["base_out"], 16 * (k.c + 1))

                with sp.Fori(0, NCH) as i:
                    for u in range(SLOTS):
                        load_edges(supertile(i, u))
                for u in range(SLOTS):
                    load_edges(supertile(NCH, u))
                sp.wait_ge(s["kv_done"], CREDIT + NCH + 1)
                load_rows(node_chunk(0))
                with sp.Fori(0, NCH - 1) as i:
                    for u in range(SLOTS):
                        load_edges(supertile(i + NCH + 1, u))
                    store_base(node_chunk(i))
                    load_rows(node_chunk(i + 1))
                load_edges(first_tail)
                load_edges(last_tail)
                store_base(node_chunk(NCH - 1))
                load_rows(tail)
                store_base(tail)

            @block.gpsimd
            def _(pool):
                def gather(k):
                    pool.wait_ge(used[k.u], CREDIT + k.q)
                    pool.wait_ge(cur_ready[k.u], k.q + 1)
                    pool.sem_inc(s["carrier"], 1)
                    for j in range(J):
                        pool.indirect_dma_start(
                            out=g_ring[k.r, k.u, j, :], out_offset=None, in_=xn_dram,
                            in_offset=bass.IndirectOffsetOnAxis(ap=cur[k.r, k.u, j:j + 1], axis=0),
                        ).then_inc(gathered[k.u], 16)

                with pool.Fori(0, ROUNDS) as i:
                    for u in range(SLOTS):
                        gather(supertile(i, u))
                gather(first_tail)
                gather(last_tail)

            @block.scalar
            def _(act):
                def stage(sup, u):
                    act.activation(cur[:, u, :], srcT[:, bass.ds(sup * J, J)], ACT.Copy).then_inc(cur_ready[u], 1)

                def relu(k):
                    act.wait_ge(summed[k.u], CREDIT + k.q + 1)
                    m = g_ring[k.r, k.u, :, :]
                    act.activation(m, m, ACT.Relu).then_inc(messages[k.u], 1)

                def edges(k):
                    relu(k)
                    stage(k.s + SLOTS, k.u)

                def stage_rows(k, users, n):
                    act.wait_ge(users, CREDIT + n)
                    act.sem_inc(s["carrier"], 1)
                    act.activation(xc[:, :, 0:k.n], xnT[:, :, bass.ds(k.c * CH, k.n)], ACT.Copy).then_inc(s["xc_ready"], 1)

                def keys_values(k, t):
                    r = slice(0, k.rows)
                    act.wait_ge(s["proj_done"], CREDIT + TILES * k.c + t + 1)
                    if t == 0:
                        act.wait_ge(s["kv_done"], CREDIT + k.c)
                    act.activation(kvraw[r, t * 2 * C:(t + 1) * 2 * C], ps[r, 2 + t % 2, :], ACT.Copy)
                    act.wait_ge(s["ssq_done"], CREDIT + TILES * k.c + t)
                    act.activation(sq[r, :], ps[r, 2 + t % 2, :], ACT.Square).then_inc(raw_done[t % 2], 1)

                for u in range(SLOTS):
                    stage(u, u)
                with act.Fori(0, NCH) as i:
                    k = node_chunk(i)
                    stage_rows(k, s["proj_done"], TILES * i)
                    edges(supertile(i, 0))
                    edges(supertile(i, 1))
                    keys_values(k, 0)
                    keys_values(k, 1)
                    edges(supertile(i, 2))
                    keys_values(k, 2)
                    keys_values(k, 3)
                    edges(supertile(i, 3))
                stage_rows(tail, s["proj_done"], TILES * NCH)
                edges(supertile(NCH, 0))
                edges(supertile(NCH, 1))
                keys_values(tail, 0)
                edges(supertile(NCH, 2))
                edges(supertile(NCH, 3))
                act.wait_ge(s["r_done"], 1)
                act.activation(rmat, ps[:, 7, :].rearrange("p (k c) -> p k c", k=KC), ACT.Copy).then_inc(s["r_copied"], 1)
                with act.Fori(0, NCH - 1) as i:
                    stage_rows(node_chunk(i), s["mixed"], i)
                    for u in range(SLOTS):
                        edges(supertile(i + NCH + 1, u))
                stage_rows(node_chunk(NCH - 1), s["mixed"], NCH - 1)
                relu(first_tail)
                stage_rows(tail, s["mixed"], NCH)
                relu(last_tail)

            @block.vector
            def _(dve):
                def add_attributes(k):
                    dve.wait_ge(gathered[k.u], 16 * J * (k.q + 1))
                    dve.wait_ge(e_in[k.u], 16 * (k.q + 1))
                    m = g_ring[k.r, k.u, :, :]
                    dve.tensor_tensor(m, m, e_ring[k.r, k.u, :, :], ALU.add).then_inc(summed[k.u], 1)

                def one_hot(k):
                    slot, n = other(k)
                    dve.wait_ge(used[slot], CREDIT + n)
                    parts = k.r.stop
                    dve.tensor_tensor(hot[k.r, k.b, :, :],
                                      iota[k.r, :].unsqueeze(1).to_broadcast([parts, J, WIN]),
                                      rel[k.r, bass.ds(k.s * J, J)].unsqueeze(2).to_broadcast([parts, J, WIN]),
                                      ALU.is_equal).then_inc(s["hot_ready"], 1)

                def window(k):
                    col = dve.value_load(bases[0:1, bass.ds(k.s, 1)], min_val=0, max_val=N - 1)
                    dve.wait_ge(used[k.u], CREDIT + k.q + 1)
                    prev = (k.u - 1, k.q + 1) if k.u else (SLOTS - 1, k.q)
                    dve.wait_ge(windowed[prev[0]], CREDIT + prev[1])
                    to = hT[:, :, bass.ds(col, WIN)]
                    dve.tensor_tensor(to, to, ps[:, k.b, 0:KC * WIN].rearrange("p (k w) -> p k w", k=KC),
                                      ALU.add).then_inc(windowed[k.u], 1)

                def squares(k, t):
                    r = slice(0, k.rows)
                    dve.wait_ge(raw_done[t % 2], CREDIT + (TILES // 2) * k.c + t // 2 + 1)
                    dve.tensor_reduce(rs[r, 0, t * 2 * NH:(t + 1) * 2 * NH], sq[r, :].rearrange("p (g d) -> p g d", d=HEAD),
                                      AX.X, ALU.add).then_inc(s["ssq_done"], 1)

                def scale_keys_values(k):
                    r, n = slice(0, k.rows), k.tiles * 2 * NH
                    steps = Steps(dve, s["kv_steps"], k.c * (1 + RSQRT_STEPS))
                    dve.wait_ge(s["ssq_done"], CREDIT + TILES * k.c + k.tiles)
                    v, y, h = (rs[r, m, 0:n] for m in range(3))
                    steps.run(dve.tensor_scalar(v, v, 1.0 / HEAD, EPS, ALU.mult, ALU.add))
                    rsqrt_steps(dve, steps, v, y, h)
                    kv = kvraw[r, 0:n * HEAD].rearrange("p (g d) -> p g d", d=HEAD)
                    dve.tensor_tensor(kv, kv, y.unsqueeze(2).to_broadcast([k.rows, n, HEAD]), ALU.mult).then_inc(s["scaled"], 1)

                def add_base(k, n):
                    r = slice(0, k.rows)
                    dve.wait_ge(s["x_in"], 16 * (k.c + 1))
                    dve.wait_ge(s["mixed"], CREDIT + k.c + 1)
                    rows = xrows[r, 0:k.tiles, :]
                    step = Steps(dve, s["am_steps"], n)
                    step.run(dve.tensor_tensor(rows, rows, ps[r, 2:4, :].rearrange("p b (t c) -> p (b t) c", c=C)[:, 0:k.tiles, :], ALU.add))
                    dve.tensor_tensor(rows, rows, bo_row[r, :].unsqueeze(1).to_broadcast([k.rows, k.tiles, C]),
                                      ALU.add).then_inc(s["base_added"], 1)

                mixing = Steps(dve, s["am_steps"])

                def key_value_sums():
                    sv, k_bias, k_col = sq[:, 0:C], tiny[:, 6, 0:1], tiny[:, 7, 0:KC]
                    dve.wait_ge(s["kv_done"], CREDIT + NCH + 1)
                    dve.wait_ge(s["vectors_in"], VECTORS)
                    dve.tensor_scalar(sv, ps[:, 6, 0:C], v_kb, None, ALU.mult)
                    mixing.run(dve.tensor_scalar(k_bias, v_kb, float(N), None, ALU.mult))
                    for p in range(KC):
                        dve.scalar_tensor_tensor(amat[:, p, :], ps[:, 4 + p, 0:P], v_kg, sv[:, p * P:(p + 1) * P],
                                                 ALU.mult, ALU.add)
                        last = dve.scalar_tensor_tensor(k_col[:, p:p + 1], ps[:, 4 + p, P:P + 1], v_kg, k_bias,
                                                        ALU.mult, ALU.add)
                    mixing.run(last)
                    for p in range(KC):
                        last = dve.tensor_tensor(amat[:, p, :], amat[:, p, :], vrow[:, 0, :], ALU.mult)
                    mixing.run(last)
                    for p in range(KC):
                        last = dve.scalar_tensor_tensor(amat[:, p, :], vrow[:, 1, :], k_col[:, p:p + 1], amat[:, p, :],
                                                        ALU.mult, ALU.add)
                    mixing.run(last)
                    mixing.run(dve.tensor_scalar(amat[:, :, :], amat[:, :, :], 1.0 / N, None, ALU.mult))
                    for p in range(KC):
                        dve.memset(amat[0:HEAD, p, HEAD:P], 0.0)
                        last = dve.memset(amat[HEAD:P, p, 0:HEAD], 0.0)
                    last.then_inc(s["am_ready"], 1)

                def add_identity():
                    dve.wait_ge(s["m_done"], 1)
                    mixing.run(dve.tensor_copy(mixm, ps[:, 7, :].rearrange("p (k c) -> p k c", k=KC)))
                    for p in range(KC):
                        d = mixm[:, p, p * P:(p + 1) * P]
                        last = dve.tensor_tensor(d, d, ident[:, :], ALU.add)
                    last.then_inc(s["m_copied"], 1)

                for b in (4, 5, 6):
                    last = dve.memset(ps[:, b, :], 0.0)
                last.then_inc(s["kv_zero"], 1)

                steps = Steps(dve, s["flag_steps"])
                f = tiny[:, 8, :]
                steps.run(dve.memset(f, 0.0))
                full, part = rel[:, 0:NST * J], rel[0:ETAIL, NST * J:NBASE * J]
                dve.tensor_reduce(f[:, 0:1], full, AX.X, ALU.max)
                dve.tensor_reduce(f[:, 1:2], full, AX.X, ALU.min)
                dve.tensor_reduce(f[0:ETAIL, 2:3], part, AX.X, ALU.max)
                steps.run(dve.tensor_reduce(f[0:ETAIL, 3:4], part, AX.X, ALU.min))
                steps.run(dve.tensor_tensor(f[:, 0:1], f[:, 0:1], f[:, 2:3], ALU.max))
                steps.run(dve.tensor_tensor(f[:, 1:2], f[:, 1:2], f[:, 3:4], ALU.min))
                steps.run(dve.tensor_scalar(f[:, 0:1], f[:, 0:1], float(1 - WIN), None, ALU.add))
                steps.run(dve.tensor_scalar(f[:, 1:2], f[:, 1:2], -1.0, None, ALU.mult))
                dve.tensor_tensor(f[:, 0:1], f[:, 0:1], f[:, 1:2], ALU.max).then_inc(s["flag_f"], 1)
                dve.wait_ge(s["flag_t"], 1)
                steps.run(dve.tensor_reduce(tiny[0:1, 9, 0:1], ps[0:1, 7, 0:P], AX.X, ALU.max))
                dve.wait_ge(s["flag_in"], 16)
                dve.tensor_scalar(flag[0:1, 0:1], tiny[0:1, 9, 0:1], 0.0, None, ALU.is_gt).then_inc(s["flag_c"], 1)

                def edges(k):
                    add_attributes(k)
                    one_hot(k)

                edges(supertile(0, 0))
                with dve.Fori(0, NCH) as i:
                    k = node_chunk(i)
                    edges(supertile(i, 1))
                    window(supertile(i, 0))
                    edges(supertile(i, 2))
                    squares(k, 0)
                    squares(k, 1)
                    window(supertile(i, 1))
                    edges(supertile(i, 3))
                    squares(k, 2)
                    squares(k, 3)
                    window(supertile(i, 2))
                    scale_keys_values(k)
                    edges(supertile(i + 1, 0))
                    window(supertile(i, 3))
                edges(supertile(NCH, 1))
                window(supertile(NCH, 0))
                squares(tail, 0)
                scale_keys_values(tail)
                edges(supertile(NCH, 2))
                window(supertile(NCH, 1))
                key_value_sums()
                edges(supertile(NCH, 3))
                window(supertile(NCH, 2))
                edges(supertile(NCH + 1, 0))
                window(supertile(NCH, 3))
                add_identity()
                n = mixing.n
                with dve.Fori(0, NCH - 1) as i:
                    edges(supertile(i + NCH + 1, 1))
                    window(supertile(i + NCH + 1, 0))
                    edges(supertile(i + NCH + 1, 2))
                    add_base(node_chunk(i), n + i)
                    window(supertile(i + NCH + 1, 1))
                    edges(supertile(i + NCH + 1, 3))
                    window(supertile(i + NCH + 1, 2))
                    edges(supertile(i + NCH + 2, 0))
                    window(supertile(i + NCH + 1, 3))
                add_base(node_chunk(NCH - 1), n + NCH - 1)
                edges(last_tail)
                window(first_tail)
                add_base(tail, n + NCH)
                window(last_tail)
                dve.wait_ge(windowed[1], CREDIT + ROUNDS + 1)

            @block.tensor
            def _(pe):
                def sum_by_destination(k):
                    pe.wait_ge(messages[k.u], k.q + 1)
                    pe.wait_ge(s["hot_ready"], k.s + 1)
                    slot, n = other(k)
                    pe.wait_ge(windowed[slot], CREDIT + n)
                    for kc in range(KC):
                        for j in range(J):
                            last = pe.matmul(ps[:, k.b, kc * WIN:(kc + 1) * WIN], g_ring[k.r, k.u, j, kc * P:(kc + 1) * P],
                                             hot[k.r, k.b, j, :], start=(kc == 0 and j == 0), stop=(j == J - 1),
                                             skip_group_check=True)
                    last.then_inc(used[k.u], 1)

                def project(k, t):
                    if t == 0:
                        pe.wait_ge(s["xc_ready"], k.c + 1)
                    pe.wait_ge(raw_done[t % 2], CREDIT + (TILES // 2) * k.c + t // 2)
                    for kc in range(KC):
                        last = pe.matmul(ps[0:k.rows, 2 + t % 2, :], xc[:, kc, t * P:t * P + k.rows], wkvT[:, kc, :],
                                         start=(kc == 0), stop=(kc == KC - 1))
                    last.then_inc(s["proj_done"], 1)

                def sum_keys_values(k):
                    pe.wait_ge(s["scaled"], k.c + 1)
                    r = slice(0, k.rows)
                    flags = dict(start=False, stop=False, skip_group_check=True)
                    for t in range(k.tiles):
                        for p in range(KC):
                            keys = kvraw[r, t * 2 * C + p * P:t * 2 * C + (p + 1) * P]
                            values = kvraw[r, t * 2 * C + C + p * P:t * 2 * C + C + (p + 1) * P]
                            pe.matmul(ps[:, 4 + p, 0:P], keys, values, **flags)
                            pe.matmul(ps[:, 4 + p, P:P + 1], keys, ones[r, 0:1], **flags)
                            last = pe.matmul(ps[:, 6, p * P:(p + 1) * P], ones[r, :], values, **flags)
                    last.then_inc(s["kv_done"], 1)

                def mix_rows(k, n):
                    pe.wait_ge(s["xc_ready"], n)
                    pe.wait_ge(s["base_added"], CREDIT + k.c)
                    for t in range(k.tiles):
                        for kc in range(KC):
                            last = pe.matmul(ps[0:k.rows, 2 + t // 2, (t % 2) * C:(t % 2 + 1) * C],
                                             xc[:, kc, t * P:t * P + k.rows], mixm[:, kc, :],
                                             start=(kc == 0), stop=(kc == KC - 1), skip_group_check=True)
                    last.then_inc(s["mixed"], 1)

                for credited in (*summed, *used, *windowed, *raw_done, s["proj_done"], s["kv_done"], s["ssq_done"], s["mixed"],
                                 s["base_added"]):
                    pe.sem_inc(credited, CREDIT)
                pe.wait_ge(s["flag_f"], 1)
                pe.transpose(ps[0:1, 7, 0:P], tiny[:, 8, 0:1], ident[:, :]).then_inc(s["flag_t"], 1)
                pe.wait_ge(s["kv_zero"], 1)
                pe.wait_ge(s["flag_c"], 1)
                with pe.Fori(0, NCH) as i:
                    k = node_chunk(i)
                    sum_by_destination(supertile(i, 0))
                    project(k, 0)
                    project(k, 1)
                    sum_by_destination(supertile(i, 1))
                    project(k, 2)
                    project(k, 3)
                    sum_by_destination(supertile(i, 2))
                    sum_by_destination(supertile(i, 3))
                    sum_keys_values(k)
                sum_by_destination(supertile(NCH, 0))
                project(tail, 0)
                sum_by_destination(supertile(NCH, 1))
                sum_keys_values(tail)
                sum_by_destination(supertile(NCH, 2))
                pe.wait_ge(s["am_ready"], 1)
                for p in range(KC):
                    last = pe.matmul(ps[:, 7, p * C:(p + 1) * C], amat[:, p, :], wq[:, p, :], start=True, stop=True)
                last.then_inc(s["r_done"], 1)
                sum_by_destination(supertile(NCH, 3))
                pe.wait_ge(s["r_copied"], 1)
                for m in range(KC):
                    for p in range(KC):
                        last = pe.matmul(ps[:, 7, m * C:(m + 1) * C], rmat[:, p, m * P:(m + 1) * P], woT[:, p, :],
                                         start=(p == 0), stop=(p == KC - 1), skip_group_check=True)
                last.then_inc(s["m_done"], 1)
                pe.wait_ge(s["m_copied"], 1)
                with pe.Fori(0, NCH - 1) as i:
                    sum_by_destination(supertile(i + NCH + 1, 0))
                    mix_rows(node_chunk(i), NCH + 1 + i + 1)
                    for u in range(1, SLOTS):
                        sum_by_destination(supertile(i + NCH + 1, u))
                mix_rows(node_chunk(NCH - 1), 2 * NCH + 1)
                sum_by_destination(first_tail)
                mix_rows(tail, 2 * NCH + 2)
                sum_by_destination(last_tail)

        gsem = {n: sem("general_" + n) for n in
                                  ("e", "g", "cur", "sum", "msg", "rel", "hot", "used", "added", "steps")}
        gcur, grel, gmask = cur[:, 0, :], tiny[:, 10:12, :].rearrange("p a b -> p (a b)"), tiny[:, 12:14, :].rearrange("p a b -> p (a b)")

        def if_outside(eng, body):
            outside = eng.value_load(flag[0:1, 0:1], min_val=0, max_val=1)
            with eng.If(outside > 0):
                body()
            eng.sem_inc(s["carrier"], 1)

        def each_supertile(eng, body):
            with eng.Fori(0, NST) as i:
                body(Supertile(i))
            body(Supertile(NST, ETAIL))

        with nc.Block() as block:
            @block.sync
            def _(sp):
                def body():
                    def load(k):
                        sp.wait_ge(gsem["added"], CREDIT + NWIN * k.s)
                        rows = edge_attr[bass.ds(k.s * ST, k.r.stop * J), :]
                        sp.dma_start(e_ring[k.r, 0, :, :], rows.rearrange("(p j) c -> p j c", j=J)).then_inc(gsem["e"], 16)
                    each_supertile(sp, load)
                if_outside(sp, body)

            @block.gpsimd
            def _(pool):
                def body():
                    def gather(k):
                        pool.wait_ge(gsem["cur"], k.s + 1)
                        pool.sem_inc(s["carrier"], 1)
                        for j in range(J):
                            pool.indirect_dma_start(
                                out=g_ring[k.r, 0, j, :], out_offset=None, in_=xn_dram,
                                in_offset=bass.IndirectOffsetOnAxis(ap=gcur[k.r, j:j + 1], axis=0)).then_inc(gsem["g"], 16)
                    each_supertile(pool, gather)
                if_outside(pool, body)

            @block.scalar
            def _(act):
                def body():
                    def relu(k):
                        act.wait_ge(gsem["added"], CREDIT + NWIN * k.s)
                        act.sem_inc(s["carrier"], 1)
                        act.activation(gcur, srcT[:, bass.ds(k.s * J, J)], ACT.Copy).then_inc(gsem["cur"], 1)
                        act.wait_ge(gsem["sum"], k.s + 1)
                        m = g_ring[k.r, 0, :, :]
                        act.activation(m, m, ACT.Relu).then_inc(gsem["msg"], 1)
                    each_supertile(act, relu)
                if_outside(act, body)

            @block.vector
            def _(dve):
                def body():
                    def add(k):
                        dve.wait_ge(gsem["g"], 16 * J * (k.s + 1))
                        dve.wait_ge(gsem["e"], 16 * (k.s + 1))
                        m = g_ring[k.r, 0, :, :]
                        dve.tensor_tensor(m, m, e_ring[k.r, 0, :, :], ALU.add).then_inc(gsem["sum"], 1)
                        steps = Steps(dve, gsem["steps"], k.s * 5)
                        col = rel[:, bass.ds(k.s * J, J)]
                        base = basebc[:, bass.ds(k.s, 1)].to_broadcast([P, J])
                        dve.tensor_scalar(gmask, col, 0.0, None, ALU.is_lt)
                        steps.run(dve.tensor_scalar(grel, col, float(WIN), None, ALU.is_ge))
                        steps.run(dve.tensor_tensor(gmask, gmask, grel, ALU.add))
                        steps.run(dve.tensor_tensor(grel, col, base, ALU.add))
                        steps.run(dve.scalar_tensor_tensor(grel, grel, 1.0, gmask, ALU.add, ALU.mult))
                        steps.run(dve.tensor_scalar(grel, grel, -1.0, None, ALU.add))

                        def window(w):
                            n = NWIN * k.s + w
                            dve.wait_ge(gsem["used"], CREDIT + n)
                            parts = k.r.stop
                            h = hot[k.r, 0, :, :]
                            dve.tensor_tensor(h, iota[k.r, :].unsqueeze(1).to_broadcast([parts, J, WIN]),
                                              grel[k.r, :].unsqueeze(2).to_broadcast([parts, J, WIN]), ALU.is_equal).then_inc(gsem["hot"], 1)
                            dve.wait_ge(gsem["hot"], n + 1)
                            dve.tensor_scalar(grel, grel, float(-WIN), None, ALU.add).then_inc(gsem["rel"], 1)
                            dve.wait_ge(gsem["rel"], n + 1)
                            dve.wait_ge(gsem["used"], CREDIT + n + 1)
                            to = hT[:, :, bass.ds(w * WIN, WIN)]
                            dve.tensor_tensor(to, to, ps[:, 0, 0:KC * WIN].rearrange("p (k w) -> p k w", k=KC),
                                              ALU.add).then_inc(gsem["added"], 1)

                        dve.sem_inc(s["carrier"], 1)
                        with dve.Fori(0, NWIN) as w:
                            window(w)
                    each_supertile(dve, add)
                    dve.wait_ge(gsem["added"], CREDIT + NWIN * NBASE)
                if_outside(dve, body)

            @block.tensor
            def _(pe):
                def body():
                    pe.sem_inc(gsem["added"], CREDIT)
                    pe.sem_inc(gsem["used"], CREDIT)

                    def sum_by_destination(k):
                        pe.wait_ge(gsem["msg"], k.s + 1)
                        pe.sem_inc(s["carrier"], 1)
                        with pe.Fori(0, NWIN) as w:
                            n = NWIN * k.s + w
                            pe.wait_ge(gsem["added"], CREDIT + n)
                            pe.wait_ge(gsem["hot"], n + 1)
                            for kc in range(KC):
                                for j in range(J):
                                    last = pe.matmul(ps[:, 0, kc * WIN:(kc + 1) * WIN], g_ring[k.r, 0, j, kc * P:(kc + 1) * P],
                                                     hot[k.r, 0, j, :], start=(kc == 0 and j == 0),
                                                     stop=(j == J - 1), skip_group_check=True)
                            last.then_inc(gsem["used"], 1)
                    each_supertile(pe, sum_by_destination)
                if_outside(pe, body)

        h1T = big[:, :].rearrange("p (m n) -> p m n", m=KH)
        h2T = hT
        w1_sb = kvraw[:, 0:KC * H].rearrange("p (k m) -> p k m", k=KC)
        w2_sb = kvraw[:, KC * H:KC * H + KH * C].rearrange("p (k m) -> p k m", k=KH)
        ew_in = ring[:, 0:2 * 2 * KC * C].rearrange("p (s n k m) -> p s n k m", s=2, n=2, k=KC)
        eb2 = sq[0:NE, 0:C]
        bn1 = xc[:, 0, :]
        bn2 = xc[:, 1, :]
        NS = (NCH + 1) * 6
        coef = rs[:, :, :].rearrange("p a b -> p (a b)")
        scale1, shift1, tmp1, mv1 = coef[:, 0:KH], coef[:, KH:2 * KH], coef[:, 2 * KH:3 * KH], coef[:, 16:16 + 2 * KH]
        g = [coef[:, 32 + KC * n:32 + KC * (n + 1)] for n in range(14)]
        m = {n: sem("mlp_" + n) for n in
                               """w1 w2 ew ew_in0 ew_in1 ln1_0 ln1_1 copied0 copied1 stats0 stats1 scale steps relu0 relu1 lin2_0 lin2_1
                               copied2_0 copied2_1 stats2 mean1 mean1c coef sum_in""".split()}

        def load_expert(sp, e):
            for n, w in enumerate((ffn["w1"], ffn["w2"])):
                sp.dma_start(ew_in[:, e % 2, n, :, :], w[e].rearrange("(k p) m -> p k m", p=P)).then_inc((m["ew_in0"], m["ew_in1"])[e % 2], 16)

        with nc.Block() as block:
            @block.sync
            def _(sp):
                sp.dma_start(w1_sb, gnn["W1"].rearrange("(k p) m -> p k m", p=P)).then_inc(m["w1"], 16)
                sp.dma_start(w2_sb, gnn["W2"].rearrange("(k p) m -> p k m", p=P)).then_inc(m["w2"], 16)
                load_expert(sp, 0)
                load_expert(sp, 1)
                sp.dma_start(eb2, ffn["b2"]).then_inc(m["ew"], 16)
                sp.wait_ge(m["ew"], 16)

            @block.tensor
            def _(pe):
                def first(k):
                    pe.wait_ge((m["copied0"], m["copied1"])[k.u], CREDIT + k.i)
                    for mt in range(KH):
                        for kc in range(KC):
                            last = pe.matmul(ps[:, 4 * k.u + mt, 0:k.n], w1_sb[:, kc, mt * P:(mt + 1) * P],
                                             hT[:, kc, bass.ds(k.c * CH, k.n)], start=(kc == 0), stop=(kc == KC - 1))
                    last.then_inc((m["ln1_0"], m["ln1_1"])[k.u], 1)

                def second(k):
                    pe.wait_ge((m["relu0"], m["relu1"])[k.u], k.i + 1)
                    pe.wait_ge((m["copied2_0"], m["copied2_1"])[k.u], CREDIT + k.i)
                    for mt in range(KC):
                        for kh in range(KH):
                            last = pe.matmul(ps[:, 2 * k.u + mt, 0:k.n], w2_sb[:, kh, mt * P:(mt + 1) * P],
                                             h1T[:, kh, bass.ds(k.c * CH, k.n)], start=(kh == 0), stop=(kh == KH - 1))
                    last.then_inc((m["lin2_0"], m["lin2_1"])[k.u], 1)

                for credited in (m["copied0"], m["copied1"], m["copied2_0"], m["copied2_1"]):
                    pe.sem_inc(credited, CREDIT)
                pe.wait_ge(m["w1"], 16)
                all_chunks(pe, first)
                pe.wait_ge(m["w2"], 16)
                all_chunks(pe, second)
                pe.wait_ge(m["sum_in"], 1)
                pe.matmul(ps[:, 6, 0:KC], ones[:, :], g[0], start=True, stop=True).then_inc(m["mean1"], 1)
                pe.wait_ge(m["sum_in"], 2)
                pe.matmul(ps[:, 7, 0:KC], ones[:, :], g[3], start=True, stop=True).then_inc(m["mean1"], 1)

            @block.scalar
            def _(act):
                def first(k):
                    act.wait_ge((m["ln1_0"], m["ln1_1"])[k.u], k.i + 1)
                    act.sem_inc(s["carrier"], 1)
                    for mt in range(KH):
                        last = act.activation(h1T[:, mt, bass.ds(k.c * CH, k.n)], ps[:, 4 * k.u + mt, 0:k.n], ACT.Identity,
                                              bias=v_b1[:, mt:mt + 1])
                    last.then_inc((m["copied0"], m["copied1"])[k.u], 1)

                def relu(k):
                    for mt in range(KH):
                        a = h1T[:, mt, bass.ds(k.c * CH, k.n)]
                        last = act.activation(a, a, ACT.Relu, bias=shift1[:, mt:mt + 1], scale=scale1[:, mt:mt + 1])
                    last.then_inc((m["relu0"], m["relu1"])[k.u], 1)

                def second(k):
                    act.wait_ge((m["lin2_0"], m["lin2_1"])[k.u], k.i + 1)
                    act.sem_inc(s["carrier"], 1)
                    for mt in range(KC):
                        last = act.activation(h2T[:, mt, bass.ds(k.c * CH, k.n)], ps[:, 2 * k.u + mt, 0:k.n], ACT.Identity,
                                              bias=v_b2[:, mt:mt + 1])
                    last.then_inc((m["copied2_0"], m["copied2_1"])[k.u], 1)

                all_chunks(act, first)
                act.wait_ge(m["scale"], 1)
                relu(chunk_of(0, 0))
                relu(chunk_of(0, 1))
                with act.Fori(0, NCH // 2 - 1) as i:
                    for u in range(2):
                        second(chunk_of(i, u))
                        relu(chunk_of(i + 1, u))
                second(chunk_of(NCH // 2 - 1, 0))
                relu(last_chunk)
                second(chunk_of(NCH // 2 - 1, 1))
                second(last_chunk)

            @block.vector
            def _(dve):
                def stats(k, a, bn, tiles, copied, done):
                    dve.wait_ge(copied[k.u], CREDIT + k.i + 1)
                    for mt in range(tiles):
                        last = dve.bn_stats(bn[:, bass.ds(k.c * 6 + mt * NS, 6)], a[:, mt, bass.ds(k.c * CH, k.n)])
                    last.then_inc(done, 1)

                all_chunks(dve, lambda k: stats(k, h1T, bn1, KH, (m["copied0"], m["copied1"]), m["stats0"]))
                dve.wait_ge(m["stats0"], NCH + 1)
                steps = Steps(dve, m["steps"])
                for mt in range(KH):
                    last = dve.bn_aggr(mv1[:, 2 * mt:2 * mt + 2], bn1[:, mt * NS:(mt + 1) * NS])
                steps.run(last)
                mean, var = (mv1.rearrange("p (m a) -> p m a", a=2)[:, :, a] for a in range(2))
                steps.run(dve.tensor_scalar(shift1, var, EPS, None, ALU.add))
                rsqrt_steps(dve, steps, shift1, scale1, tmp1)
                steps.run(dve.tensor_tensor(scale1, scale1, v_gamma, ALU.mult))
                steps.run(dve.tensor_tensor(tmp1, scale1, mean, ALU.mult))
                dve.tensor_tensor(shift1, v_beta, tmp1, ALU.subtract).then_inc(m["scale"], 1)

                all_chunks(dve, lambda k: stats(k, h2T, bn2, KC, (m["copied2_0"], m["copied2_1"]), m["stats1"]))
                dve.wait_ge(m["stats1"], NCH + 1)
                mv2 = coef[:, 16 + 2 * KH:16 + 2 * KH + 2 * KC]
                for mt in range(KC):
                    last = dve.bn_aggr(mv2[:, 2 * mt:2 * mt + 2], bn2[:, mt * NS:(mt + 1) * NS])
                steps.run(last)
                mean, var = (mv2.rearrange("p (m a) -> p m a", a=2)[:, :, a] for a in range(2))
                dve.tensor_copy(g[0], mean).then_inc(m["sum_in"], 1)
                dve.wait_ge(m["mean1"], 1)
                steps.run(dve.tensor_copy(g[1], ps[:, 6, 0:KC]))
                steps.run(dve.tensor_reduce(g[2][:, 0:1], g[1], AX.X, ALU.add))
                steps.run(dve.tensor_scalar(g[2][:, 0:1], g[2][:, 0:1], 1.0 / C, None, ALU.mult))
                mean_g = g[2][:, 0:1]
                steps.run(dve.tensor_scalar(g[1], mean, mean_g, None, ALU.subtract))
                steps.run(dve.tensor_tensor(g[3], g[1], g[1], ALU.mult))
                dve.tensor_tensor(g[3], g[3], var, ALU.add).then_inc(m["sum_in"], 1)
                dve.wait_ge(m["mean1"], 2)
                steps.run(dve.tensor_copy(g[4], ps[:, 7, 0:KC]))
                steps.run(dve.tensor_reduce(g[5][:, 0:1], g[4], AX.X, ALU.add))
                steps.run(dve.tensor_scalar(g[5][:, 0:1], g[5][:, 0:1], 1.0 / C, EPS, ALU.mult, ALU.add))
                rsqrt_steps(dve, steps, g[5][:, 0:1], g[6][:, 0:1], g[6][:, 1:2])
                a1, b1, m1, v1 = g[7], g[8], g[9], g[10]
                steps.run(dve.tensor_scalar(a1, v_lnw, g[6][:, 0:1], None, ALU.mult))
                steps.run(dve.tensor_tensor(m1, g[1], a1, ALU.mult))
                steps.run(dve.tensor_tensor(m1, m1, v_lnb, ALU.add))
                steps.run(dve.tensor_scalar(b1, a1, mean_g, None, ALU.mult))
                steps.run(dve.tensor_tensor(b1, v_lnb, b1, ALU.subtract))
                steps.run(dve.tensor_tensor(v1, a1, a1, ALU.mult))
                steps.run(dve.tensor_tensor(v1, v1, var, ALU.mult))
                steps.run(dve.tensor_tensor(g[11], m1, v_gnms, ALU.mult))
                steps.run(dve.tensor_tensor(g[12], m1, g[11], ALU.subtract))
                steps.run(dve.tensor_tensor(g[12], g[12], g[12], ALU.mult))
                steps.run(dve.tensor_tensor(v1, v1, g[12], ALU.add))
                steps.run(dve.tensor_scalar(v1, v1, EPS, None, ALU.add))
                rsqrt_steps(dve, steps, v1, g[12], g[13])
                steps.run(dve.tensor_tensor(g[12], g[12], v_gnw, ALU.mult))
                steps.run(dve.tensor_tensor(g[11], b1, g[11], ALU.subtract))
                steps.run(dve.tensor_tensor(g[11], g[11], g[12], ALU.mult))
                steps.run(dve.tensor_tensor(shift1[:, 0:KC], g[11], v_gnb, ALU.add))
                steps.run(dve.tensor_tensor(scale1[:, 0:KC], a1, g[12], ALU.mult))

        until_ffn.close()
        off = [0]

        def part(n):
            off[0] += n
            assert off[0] <= SLOTS * J * C + KC * 2 * C
            place = ring if off[0] <= SLOTS * J * C else wkvT[:, :, :].rearrange("p k c -> p (k c)")
            at = off[0] - (0 if off[0] <= SLOTS * J * C else SLOTS * J * C)
            return place[:, at - n:at]

        part(2 * 2 * KC * C)
        gnnT = part(KC * CH).rearrange("p (k n) -> p k n", k=KC)
        base_in = [part(TILES * C).rearrange("p (t c) -> p t c", t=TILES) for _ in range(2)]
        tok = part(TILES * C).rearrange("p (t c) -> p t c", t=TILES)
        acc = [part(TILES * C).rearrange("p (t c) -> p t c", t=TILES) for _ in range(2)]
        comb = [part(TILES * NE).rearrange("p (t e) -> p t e", t=TILES) for _ in range(2)]
        combT = part(CH)[0:NE, :]
        logit, top, top_f, pick = (part(TILES * NE).rearrange("p (t e) -> p t e", t=TILES) for _ in range(4))
        top_i = part(TILES * NE).bitcast(U32).rearrange("p (t e) -> p t e", t=TILES)
        order = part(NE)
        tokT = xc
        hidT = [kvraw[:, n * KC * CH:(n + 1) * KC * CH].rearrange("p (k n) -> p k n", k=KC) for n in range(2)]
        tok_hi, tok_lo, hid_hi, hid_lo = ([sb(f"{name}{u}", [P, KC, CH], F32R) for u in range(2)]
                                          for name in ("tok_hi", "tok_lo", "hid_hi", "hid_lo"))
        ew1_hi, ew1_lo, ew2_hi, ew2_lo = (sb(name, [P, NE, KC, C], F32R) for name in ("ew1_hi", "ew1_lo", "ew2_hi", "ew2_lo"))

        def products(hi_a, lo_a, hi_b, lo_b):
            return ((hi_a, hi_b), (hi_a, lo_b), (lo_a, hi_b))

        f = {n: sem("ffn_" + n) for n in
                               """base0 base1 relu turned x1 normed steps tok_turned tok_copied routed top_ready share
                               combined comb_turned comb_copied b2_done acc_ready l1 hidden l2 added out0 out1 stored0 stored1 iota tok_lo hid_lo w_hi w_split""".split()}
        PREP_STEPS = 2 + (STATS_STEPS - 1) + 4 + 2

        with nc.Block() as block:
            @block.sync
            def _(sp):
                def load(k):
                    sp.wait_ge(f["x1"], k.c - 1)
                    sp.dma_start(base_in[k.u][0:k.rows, 0:k.tiles, :], chunk(base_dram, k.c, k.n)).then_inc((f["base0"], f["base1"])[k.u], 16)

                def store(k):
                    sp.wait_ge(f["added"], CREDIT + NE * (k.c + 1))
                    sp.dma_start(chunk(out, k.c, k.n), acc[k.u][0:k.rows, 0:k.tiles, :]).then_inc((f["out0"], f["out1"])[k.u], 16)

                for u in range(2):
                    sp.dma_start(base_in[u], chunk(base_dram, u)).then_inc((f["base0"], f["base1"])[u], 16)
                for e in range(2, NE):
                    sp.wait_ge(f["w_split"], 2 * (e - 1))
                    load_expert(sp, e)
                with sp.Fori(0, NCH // 2 - 1) as i:
                    for u in range(2):
                        load(chunk_of(i + 1, u))
                        store(chunk_of(i, u))
                        sp.wait_ge((f["out0"], f["out1"])[u], 16 * (i + 1))
                        sp.sem_inc((f["stored0"], f["stored1"])[u], 1)
                load(last_chunk)
                store(chunk_of(NCH // 2 - 1, 0))
                sp.wait_ge(f["out0"], 16 * (NCH // 2))
                sp.sem_inc(f["stored0"], 1)
                store(chunk_of(NCH // 2 - 1, 1))
                store(last_chunk)
                sp.wait_ge(f["out0"], 16 * (NCH // 2 + 1))
                sp.wait_ge(f["out1"], 16 * (NCH // 2))

            @block.gpsimd
            def _(pool):
                pool.iota(order, [[1, NE]], base=0, channel_multiplier=0,
                          allow_small_or_imprecise_dtypes=True).then_inc(f["iota"], 1)
                for e in range(NE):
                    for n, (hi, lo) in enumerate(((ew1_hi, ew1_lo), (ew2_hi, ew2_lo))):
                        w = ew_in[:, e % 2, n]
                        pool.wait_ge((m["ew_in0"], m["ew_in1"])[e % 2], 32 * (e // 2 + 1))
                        pool.tensor_copy(hi[:, e], w).then_inc(f["w_hi"], 1)
                        pool.wait_ge(f["w_hi"], 2 * e + n + 1)
                        pool.tensor_tensor(lo[:, e], w, hi[:, e].bitcast(F32), ALU.subtract).then_inc(f["w_split"], 1)

            def with_next(eng, body):
                with eng.Fori(0, NCH // 2 - 1) as i:
                    body(chunk_of(i, 0), chunk_of(i, 1))
                    body(chunk_of(i, 1), chunk_of(i + 1, 0))
                h = NCH // 2 - 1
                body(chunk_of(h, 0), chunk_of(h, 1))
                body(chunk_of(h, 1), last_chunk)
                body(last_chunk, None)

            @block.scalar
            def _(act):
                def relu(k):
                    act.wait_ge(f["turned"], CREDIT + k.c)
                    act.sem_inc(s["carrier"], 1)
                    for kc in range(KC):
                        last = act.activation(gnnT[:, kc, 0:k.n], h2T[:, kc, bass.ds(k.c * CH, k.n)], ACT.Relu,
                                              bias=shift1[:, kc:kc + 1], scale=scale1[:, kc:kc + 1])
                    last.then_inc(f["relu"], 1)

                def copy_tokens(k):
                    act.wait_ge(f["tok_turned"], CREDIT + k.c + 1)
                    for kc in range(KC):
                        act.activation(tokT[:, kc, 0:k.n], ps[:, kc, 0:k.n], ACT.Copy)
                        last = act.activation(tok_hi[k.u][:, kc, 0:k.n], ps[:, kc, 0:k.n], ACT.Copy)
                    last.then_inc(f["tok_copied"], 1)

                def share(k):
                    act.wait_ge(f["top_ready"], k.c + 1)
                    a = tiny[0:k.rows, 6, 0:k.tiles]
                    act.activation(a, a, ACT.Tanh, scale=0.5).then_inc(f["share"], 1)

                def copy_comb(k):
                    act.wait_ge(f["comb_turned"], k.c + 1)
                    act.activation(combT[:, 0:k.n], ps[0:NE, 2, 0:k.n], ACT.Copy).then_inc(f["comb_copied"], 1)

                def expert(k, e):
                    for mt in range(KC):
                        act.wait_ge(f["l1"], 2 * NE * k.c + 2 * e + mt + 1)
                        if mt == 0:
                            act.wait_ge(f["l2"], CREDIT + NE * k.c + max(e - 1, 0))
                        for hidden in (hidT[e % 2], hid_hi[e % 2]):
                            last = act.activation(hidden[:, mt, 0:k.n], ps[:, 3 + mt, 0:k.n], ACT.Gelu, bias=v_eb1[:, e, mt:mt + 1])
                        last.then_inc(f["hidden"], 1)

                def body(k, nxt):
                    if nxt:
                        relu(nxt)
                    for e in range(NE):
                        expert(k, e)
                        if nxt and e == 4:
                            copy_tokens(nxt)
                        if nxt and e == 6:
                            share(nxt)
                        if nxt and e == 7:
                            copy_comb(nxt)

                k = chunk_of(0, 0)
                relu(k), copy_tokens(k), share(k), copy_comb(k)
                with_next(act, body)

            @block.vector
            def _(dve):
                def steps_of(k, n):
                    steps = Steps(dve, f["steps"], k.c * PREP_STEPS)
                    steps.n = n
                    return steps

                def x1(k):
                    r, t = slice(0, k.rows), slice(0, k.tiles)
                    steps = steps_of(k, 0)
                    dve.wait_ge((f["base0"], f["base1"])[k.u], 16 * (k.i + 1))
                    dve.wait_ge(f["turned"], CREDIT + k.c + 1)
                    b = base_in[k.u][r, t, :]
                    steps.run(dve.tensor_tensor(b, b, ps[r, 0:2, :].rearrange("p b (t c) -> p (b t) c", c=C)[:, t, :], ALU.add))
                    for j in range(k.tiles):
                        last = dve.bn_stats(st[r, 0, j, :], base_in[k.u][r, j, :])
                    steps.run(last)
                    return steps.n

                def norm_stats(k, n):
                    r, t = slice(0, k.rows), slice(0, k.tiles)
                    steps = steps_of(k, n)
                    stats_steps(dve, steps, st[r, 0, t, :], tiny[r, 2, t], tiny[r, 4, t], tiny[r, 5, t], C, tiny[r, 3, t])
                    return steps.n

                def tokens(k, n):
                    r, t = slice(0, k.rows), slice(0, k.tiles)
                    steps = steps_of(k, n)
                    dve.wait_ge(f["tok_turned"], CREDIT + k.c)
                    for j in range(k.tiles):
                        last = dve.tensor_scalar(tok[r, j, :], base_in[k.u][r, j, :], tiny[r, 2, j:j + 1], tiny[r, 3, j:j + 1],
                                                 ALU.subtract, ALU.mult)
                    last.then_inc(f["normed"], 1)
                    dve.wait_ge(f["normed"], k.c + 1)
                    dve.wait_ge((f["stored0"], f["stored1"])[k.u], CREDIT + k.i)
                    dve.tensor_tensor(acc[k.u][r, t, :], base_in[k.u][r, t, :], tok[r, t, :], ALU.add).then_inc(f["x1"], 1)
                    return steps.n

                def choose(k, n):
                    r, t = slice(0, k.rows), slice(0, k.tiles)
                    steps = steps_of(k, n)
                    dve.wait_ge(f["routed"], k.c + 1)
                    steps.run(dve.tensor_copy(logit[r, t, :], ps[r, 2, 0:k.tiles * NE].rearrange("p (t e) -> p t e", e=NE)))
                    dve.sem_inc(s["carrier"], 1)
                    for j in range(k.tiles):
                        last = dve.max(top[r, j, :], logit[r, j, :])
                    steps.run(last)
                    dve.sem_inc(s["carrier"], 1)
                    for j in range(k.tiles):
                        last = dve.max_index(top_i[r, j, :], top[r, j, :], logit[r, j, :])
                    steps.run(last)
                    dve.tensor_tensor(tiny[r, 6, t], top[r, t, 0], top[r, t, 1], ALU.subtract).then_inc(f["top_ready"], 1)
                    steps.run(dve.tensor_copy(top_f[r, t, 0:2], top_i[r, t, 0:2]))
                    return steps.n

                def combine(k, n):
                    r, t = slice(0, k.rows), slice(0, k.tiles)
                    steps = steps_of(k, n)
                    shape = [k.rows, k.tiles, NE]
                    dve.wait_ge(f["share"], k.c + 1)
                    th, w0, w1 = tiny[r, 6, t], tiny[r, 7, t], tiny[r, 8, t]
                    dve.tensor_scalar(w0, th, 0.5, 0.5, ALU.mult, ALU.add)
                    dve.tensor_scalar(w1, th, -0.5, 0.5, ALU.mult, ALU.add)
                    dve.tensor_tensor(pick[r, t, :], order[r, :].unsqueeze(1).to_broadcast(shape),
                                      top_f[r, t, 1:2].to_broadcast(shape), ALU.is_equal)
                    steps.run(dve.tensor_tensor(comb[k.u][r, t, :], order[r, :].unsqueeze(1).to_broadcast(shape),
                                                top_f[r, t, 0:1].to_broadcast(shape), ALU.is_equal))
                    dve.tensor_tensor(pick[r, t, :], pick[r, t, :], w1.unsqueeze(2).to_broadcast(shape), ALU.mult)
                    steps.run(dve.tensor_tensor(comb[k.u][r, t, :], comb[k.u][r, t, :], w0.unsqueeze(2).to_broadcast(shape), ALU.mult))
                    dve.tensor_tensor(comb[k.u][r, t, :], comb[k.u][r, t, :], pick[r, t, :], ALU.add).then_inc(f["combined"], 1)
                    return steps.n

                def add_bias(k, n):
                    r, t = slice(0, k.rows), slice(0, k.tiles)
                    dve.wait_ge(f["b2_done"], k.c + 1)
                    a = acc[k.u][r, t, :]
                    dve.tensor_tensor(a, a, ps[r, 0:2, :].rearrange("p b (t c) -> p (b t) c", c=C)[:, t, :], ALU.add).then_inc(f["acc_ready"], 1)
                    assert n == PREP_STEPS, n

                def low_tokens(k):
                    dve.wait_ge(f["tok_copied"], k.c + 1)
                    dve.tensor_tensor(tok_lo[k.u][:, :, 0:k.n], tokT[:, :, 0:k.n], tok_hi[k.u][:, :, 0:k.n].bitcast(F32),
                                      ALU.subtract).then_inc(f["tok_lo"], 1)

                def low_hidden(k, e):
                    for mt in range(KC):
                        dve.wait_ge(f["hidden"], 2 * NE * k.c + 2 * e + mt + 1)
                        dve.tensor_tensor(hid_lo[e % 2][:, mt, 0:k.n], hidT[e % 2][:, mt, 0:k.n], hid_hi[e % 2][:, mt, 0:k.n].bitcast(F32),
                                          ALU.subtract).then_inc(f["hid_lo"], 1)

                def expert(k, e):
                    r = slice(0, k.rows)
                    dve.wait_ge(f["l2"], CREDIT + NE * k.c + e + 1)
                    dve.wait_ge(f["added"], CREDIT + NE * k.c + e)
                    if e == 0:
                        dve.wait_ge(f["acc_ready"], CREDIT + k.c + 1)
                    for j in range(k.tiles):
                        a = acc[k.u][r, j, :]
                        last = dve.scalar_tensor_tensor(a, ps[r, 5 + j // 2, (j % 2) * C:(j % 2 + 1) * C], comb[k.u][r, j, e:e + 1], a,
                                                        ALU.mult, ALU.add)
                    last.then_inc(f["added"], 1)

                def body(k, nxt):
                    n = 0
                    low_hidden(k, 0)
                    for e in range(NE):
                        if e + 1 < NE:
                            low_hidden(k, e + 1)
                        expert(k, e)
                        if nxt and e == 0:
                            n = x1(nxt)
                        if nxt and e == 1:
                            n = norm_stats(nxt, n)
                        if nxt and e == 2:
                            n = tokens(nxt, n)
                        if nxt and e == 4:
                            low_tokens(nxt)
                            n = choose(nxt, n)
                        if nxt and e == 5:
                            n = combine(nxt, n)
                        if nxt and e == 7:
                            add_bias(nxt, n)

                dve.wait_ge(f["iota"], 1)
                k = chunk_of(0, 0)
                n = x1(k)
                n = tokens(k, norm_stats(k, n))
                low_tokens(k)
                n = combine(k, choose(k, n))
                add_bias(k, n)
                with_next(dve, body)

            @block.tensor
            def _(pe):
                def turn(k):
                    pe.wait_ge(f["relu"], k.c + 1)
                    pe.wait_ge(f["acc_ready"], CREDIT + k.c)
                    for t in range(k.tiles):
                        for kc in range(KC):
                            last = pe.transpose(ps[0:k.rows, t // 2, (t % 2) * C + kc * P:(t % 2) * C + (kc + 1) * P],
                                                gnnT[:, kc, t * P:t * P + k.rows], ident[:, :])
                    last.then_inc(f["turned"], 1)

                def turn_tokens(k):
                    pe.wait_ge(f["normed"], k.c + 1)
                    for t in range(k.tiles):
                        for kc in range(KC):
                            last = pe.transpose(ps[:, kc, t * P:t * P + k.rows], tok[0:k.rows, t, kc * P:(kc + 1) * P],
                                                ident[0:k.rows, 0:k.rows])
                    last.then_inc(f["tok_turned"], 1)

                def route(k):
                    pe.wait_ge(f["tok_copied"], k.c + 1)
                    for t in range(k.tiles):
                        for kc in range(KC):
                            last = pe.matmul(ps[0:k.rows, 2, t * NE:(t + 1) * NE], tokT[:, kc, t * P:t * P + k.rows],
                                             v_rw[:, kc, :], start=(kc == 0), stop=(kc == KC - 1), skip_group_check=True)
                    last.then_inc(f["routed"], 1)

                def turn_comb(k):
                    pe.wait_ge(f["combined"], k.c + 1)
                    for t in range(k.tiles):
                        last = pe.transpose(ps[0:NE, 2, t * P:t * P + k.rows], comb[k.u][0:k.rows, t, :],
                                            ident[0:k.rows, 0:k.rows])
                    last.then_inc(f["comb_turned"], 1)

                def bias(k):
                    pe.wait_ge(f["comb_copied"], k.c + 1)
                    for t in range(k.tiles):
                        last = pe.matmul(ps[0:k.rows, t // 2, (t % 2) * C:(t % 2 + 1) * C], combT[:, t * P:t * P + k.rows],
                                         eb2, start=True, stop=True)
                    last.then_inc(f["b2_done"], 1)

                def layer1(k, e):
                    if e == 0:
                        pe.wait_ge(f["tok_lo"], k.c + 1)
                    pe.wait_ge(f["w_split"], 2 * e + 2)
                    for mt in range(KC):
                        if e > 0:
                            pe.wait_ge(f["hidden"], 2 * NE * k.c + 2 * (e - 1) + mt + 1)
                        m = slice(mt * P, (mt + 1) * P)
                        terms = [(w[:, e, kc, m], x[:, kc, 0:k.n]) for kc in range(KC)
                                 for w, x in products(ew1_hi, ew1_lo, tok_hi[k.u], tok_lo[k.u])]
                        for n, (w, x) in enumerate(terms):
                            last = pe.matmul(ps[:, 3 + mt, 0:k.n], w, x, start=(n == 0), stop=(n == len(terms) - 1))
                        last.then_inc(f["l1"], 1)

                def layer2(k, e):
                    pe.wait_ge(f["hidden"], 2 * NE * k.c + 2 * e + 2)
                    pe.wait_ge(f["hid_lo"], 2 * NE * k.c + 2 * e + 2)
                    pe.wait_ge(f["added"], CREDIT + NE * k.c + e)
                    for t in range(k.tiles):
                        terms = [(h[:, kc, t * P:t * P + k.rows], w[:, e, kc, :]) for kc in range(KC)
                                 for h, w in products(hid_hi[e % 2], hid_lo[e % 2], ew2_hi, ew2_lo)]
                        for n, (h, w) in enumerate(terms):
                            last = pe.matmul(ps[0:k.rows, 5 + t // 2, (t % 2) * C:(t % 2 + 1) * C], h, w,
                                             start=(n == 0), stop=(n == len(terms) - 1), skip_group_check=True)
                    last.then_inc(f["l2"], 1)

                def body(k, nxt):
                    layer1(k, 0)
                    if nxt:
                        turn(nxt)
                    for e in range(NE):
                        if e + 1 < NE:
                            layer1(k, e + 1)
                        if nxt and e == 7:
                            turn_comb(nxt)
                        layer2(k, e)
                        if nxt and e == 3:
                            turn_tokens(nxt)
                        if nxt and e == 4:
                            route(nxt)
                    if nxt:
                        bias(nxt)

                for credited in (f["turned"], f["l2"], f["tok_turned"], f["added"], f["acc_ready"], f["stored0"], f["stored1"]):
                    pe.sem_inc(credited, CREDIT)
                k = chunk_of(0, 0)
                turn(k), turn_tokens(k), route(k), turn_comb(k), bias(k)
                with_next(pe, body)


_INS = ['x', 'src', 'dst', 'edge_attr_256', 'L0_gnn_W1', 'L0_gnn_b1', 'L0_gnn_bn_gamma', 'L0_gnn_bn_beta', 'L0_gnn_W2',
        'L0_gnn_b2', 'L0_gnn_ln_w', 'L0_gnn_ln_b', 'L0_gnn_gn_w', 'L0_gnn_gn_b', 'L0_gnn_gn_ms', 'L0_mix_wq', 'L0_mix_wk',
        'L0_mix_wv', 'L0_mix_wo', 'L0_mix_bo', 'L0_mix_ln_k_g', 'L0_mix_ln_k_b', 'L0_mix_ln_v_g', 'L0_mix_ln_v_b',
        'L0_ffn_router_w', 'L0_ffn_w1', 'L0_ffn_b1', 'L0_ffn_w2', 'L0_ffn_b2']


def program(nc, a, out):
    def group(prefix):
        return {n[len(prefix):]: v for n, v in a.items() if n.startswith(prefix)}
    build(nc, a["x"], a["src"], a["dst"], a["edge_attr_256"], group("L0_gnn_"), group("L0_mix_"), group("L0_ffn_"), out)


def kernel(**inputs):
    import numpy as _np
    import concourse.bacc as _bacc
    from concourse import mybir as _mybir
    from concourse.bass_utils import run_bass_kernel_spmd as _run

    nc = _bacc.Bacc("TRN2", target_bir_lowering=False, num_devices=1)
    arrays, args = {}, {}
    for name in _INS:
        a = _np.ascontiguousarray(inputs[name])
        arrays[f"in_{name}_dram"] = a
        args[name] = nc.dram_tensor(f"in_{name}_dram", a.shape, _mybir.dt.from_np(a.dtype), kind="ExternalInput").ap()
    out = nc.dram_tensor("out_0_dram", args["x"].shape, _mybir.dt.float32, kind="ExternalOutput").ap()
    program(nc, args, out)
    r = _run(nc, [arrays], core_ids=[0])
    return r.results[0]["out_0_dram"]
```

```python
from contextlib import ExitStack

import concourse.bass as bass
from concourse import mybir

ALU = mybir.AluOpType
ACT = mybir.ActivationFunctionType
AX = mybir.AxisListType
F32 = mybir.dt.float32
F32R = mybir.dt.float32r
I32 = mybir.dt.int32
U32 = mybir.dt.uint32

P = 128
EPS = 1e-5
HEAD = 64
SLOTS = 4
J = 8
WIN = 160
TILES = 4
CH = TILES * P
CREDIT = 1
RSQRT_MAGIC = 0x5F3759DF
RSQRT_STEPS = 11
STATS_STEPS = 4 + RSQRT_STEPS


class Chunk:

    def __init__(self, c, n, i=None, u=None):
        self.c, self.n, self.i, self.u = c, n, i, u
        self.rows, self.tiles = min(n, P), (n + P - 1) // P


class Supertile:

    def __init__(self, s, parts=P, q=None, u=0):
        self.s, self.q, self.u, self.r, self.b = s, q, u, slice(0, parts), u % 2


class Steps:

    def __init__(self, eng, sem, base=0):
        self.eng, self.sem, self.base, self.n = eng, sem, base, 0

    def run(self, ins):
        self.n += 1
        ins.then_inc(self.sem, 1)
        self.eng.wait_ge(self.sem, self.base + self.n)


def rsqrt_steps(dve, steps, v, y, h):
    vi, yi = v.bitcast(I32), y.bitcast(I32)
    steps.run(dve.tensor_scalar(yi, vi, 1, None, ALU.logical_shift_right))
    steps.run(dve.tensor_scalar(yi, yi, -1.0, float(RSQRT_MAGIC), ALU.mult, ALU.add))
    for _ in range(3):
        steps.run(dve.scalar_tensor_tensor(h, y, -0.5, y, ALU.mult, ALU.mult))
        steps.run(dve.tensor_tensor(h, h, v, ALU.mult))
        steps.run(dve.scalar_tensor_tensor(y, h, 1.5, y, ALU.add, ALU.mult))


def stats_steps(dve, steps, st, mean, var, tmp, C, rstd):
    dve.tensor_tensor(mean, st[:, :, 1], st[:, :, 4], ALU.add)
    dve.tensor_tensor(tmp, st[:, :, 1], st[:, :, 4], ALU.subtract)
    steps.run(dve.tensor_tensor(var, st[:, :, 2], st[:, :, 5], ALU.add))
    dve.tensor_scalar(mean, mean, 0.5, None, ALU.mult)
    dve.tensor_scalar(var, var, 1.0 / C, EPS, ALU.mult, ALU.add)
    steps.run(dve.scalar_tensor_tensor(tmp, tmp, 0.25, tmp, ALU.mult, ALU.mult))
    steps.run(dve.tensor_tensor(var, var, tmp, ALU.add))
    rsqrt_steps(dve, steps, var, rstd, tmp)




def build(nc, x, src, dst, edge_attr, gnn, mix, ffn, out):
    N, C = x.shape
    E = edge_attr.shape[0]
    H = gnn["W1"].shape[1]
    NE = ffn["w1"].shape[0]
    KC = C // P
    KH = H // P
    NCH = N // CH
    TAIL = N - NCH * CH
    ST = P * J
    NST = E // ST
    ETAIL = (E - NST * ST) // J
    NBASE = NST + 1
    NCOL = NST + SLOTS - NST % SLOTS
    ROUNDS = NST // SLOTS
    NWIN = (N + WIN - 1) // WIN
    AGG = max(NWIN * WIN, N + WIN)
    NH = C // HEAD
    assert TAIL <= P and NST * ST + ETAIL * J == E and ROUNDS == 2 * NCH and NCH % 2 == 0
    assert NCOL > NST + 1

    xn_dram = nc.dram_tensor("xn_rows", [N, C], F32).ap()
    base_dram = nc.dram_tensor("base_rows", [N, C], F32).ap()

    ctx = ExitStack()
    with ctx:
        ctx.enter_context(nc.allow_non_contiguous_dma(reason="small vectors and tables"))

        def sb(name, shape, dt=F32):
            return ctx.enter_context(nc.sbuf_tensor(name, shape, dt))

        def sem(name):
            return ctx.enter_context(nc.semaphore(name))

        hT = sb("hT", [P, KC, AGG])
        kvraw = sb("kvraw", [P, TILES * 2 * C])
        wkvT = sb("wkvT", [P, KC, 2 * C])
        xc = sb("xc", [P, KC, CH])
        sq = sb("sq", [P, 2 * C])
        wq = sb("wq", [P, KC, C])
        woT = sb("woT", [P, KC, C])
        ident = sb("ident", [P, P])
        ones = sb("ones", [P, P])
        centre = kvraw[:, 0:P]
        amat = wkvT[:, 1, 0:KC * P].rearrange("p (k c) -> p k c", k=KC)
        vrow = sb("vrow", [P, 2, P])
        bo_row = sb("bo_row", [P, C])
        iota = sb("iota", [P, WIN])
        basebc = sb("basebc", [P, NCOL])
        bases = sb("bases", [1, NCOL], I32)
        flag = sb("flag", [1, 2], I32)
        vec = sb("vec", [P, 80])
        st = sb("st", [P, 2, TILES, 6])
        tiny = sb("tiny", [P, 16, TILES])
        rs = sb("rs", [P, 3, TILES * 2 * NH])
        until_ffn = ctx.enter_context(ExitStack())
        big = until_ffn.enter_context(nc.sbuf_tensor("big", [P, KH * N], F32))
        until_mlp = ctx.enter_context(ExitStack())
        ring = until_mlp.enter_context(nc.sbuf_tensor("ring", [P, SLOTS * J * C], F32))
        ps = ctx.enter_context(nc.psum_tensor("ps", [P, 8, CH], F32))

        xnT = big[:, 0:KC * N].rearrange("p (k n) -> p k n", k=KC)
        o = KC * N
        e_ring = big[:, o:o + SLOTS * J * C].rearrange("p (s j c) -> p s j c", s=SLOTS, j=J)
        o += SLOTS * J * C
        hot = big[:, o:o + 2 * J * WIN].rearrange("p (s j w) -> p s j w", s=2, j=J)
        o += 2 * J * WIN
        srcT = big[:, o:o + NCOL * J].bitcast(U32)
        o += NCOL * J
        rel = big[:, o:o + NCOL * J]
        o += NCOL * J
        cur = big[:, o:o + SLOTS * J].bitcast(U32).rearrange("p (s j) -> p s j", s=SLOTS)
        o += SLOTS * J
        assert o <= KH * N
        g_ring = ring[:, :].rearrange("p (s j c) -> p s j c", s=SLOTS, j=J)

        CR = TILES * C
        rows_in = [ring[:, n * CR:(n + 1) * CR].rearrange("p (t c) -> p t c", t=TILES) for n in range(SLOTS)]
        rows_xn = [ring[:, (SLOTS + n) * CR:(SLOTS + n + 1) * CR].rearrange("p (t c) -> p t c", t=TILES) for n in range(SLOTS)]
        ea = big[:, KC * N:KC * N + SLOTS * J * C]
        idx_i = [ea[0:NBASE, k * ST:(k + 1) * ST].bitcast(I32) for k in range(2)]
        idx_f = [ea[0:NBASE, (2 + k) * ST:(3 + k) * ST] for k in range(2)]
        wk_in = ea[:, 4 * ST:4 * ST + KC * C].rearrange("p (k c) -> p k c", k=KC)
        wv_in = ea[:, 4 * ST + KC * C:4 * ST + 2 * KC * C].rearrange("p (k c) -> p k c", k=KC)
        wo_in = ea[:, 4 * ST + 2 * KC * C:4 * ST + 3 * KC * C].rearrange("p (k c) -> p k c", k=KC)
        rw_in = ea[0:NE, 4 * ST + 3 * KC * C:4 * ST + 3 * KC * C + C]

        base_row = kvraw[0:1, 2 * P:2 * P + NBASE]

        at = [0]

        def cols(n):
            at[0] += n
            assert at[0] <= 80
            return vec[:, at[0] - n:at[0]]

        v_b1, v_gamma, v_beta = cols(KH), cols(KH), cols(KH)
        v_b2, v_lnw, v_lnb, v_gnw, v_gnb, v_gnms = (cols(KC) for _ in range(6))
        v_kg, v_kb = cols(1), cols(1)
        v_eb1 = cols(NE * KC).rearrange("p (e k) -> p e k", e=NE)
        v_rw = cols(KC * NE).rearrange("p (k e) -> p k e", k=KC)
        s = {name: sem(name) for name in """vectors_in tables_in weights_in rows_in0 rows_in1 rows_in2 rows_in3 rows_done
                rows_out0 rows_out1 rows_out2 rows_out3 turned copied table_steps dve_steps const_pool const_done table_f table_t table_done
                weight_t weight_done w1_in carrier flag_in flag_t flag_c
                e_in0 e_in1 e_in2 e_in3 gathered0 gathered1 gathered2 gathered3 cur0 cur1 cur2 cur3
                summed0 summed1 summed2 summed3 relu0 relu1 relu2 relu3 used0 used1 used2 used3
                windowed0 windowed1 windowed2 windowed3 hot_ready kv_steps
                xc_ready proj_done raw_done ssq_done scaled kv_done am_steps am_ready r_done r_copied m_done m_copied
                mixed x_in base_added base_out kv_zero base_f base_t flag_f flag_steps raw_done1""".split()}
        VECTORS = 16 * (9 + 4 + 2 + 4)
        four = lambda name: [s[f"{name}{k}"] for k in range(SLOTS)]

        def chunk(a, c, n=CH):
            if n == CH:
                return a[bass.ds(c * CH, CH), :].rearrange("(t p) c -> p t c", p=P)
            return a[NCH * CH:N, :].rearrange("(t p) c -> p t c", t=1)

        def chunk_of(i, u):
            return Chunk(2 * i + u, CH, i, u)

        last_chunk = Chunk(NCH, TAIL, NCH // 2, 0)

        def all_chunks(eng, body):
            with eng.Fori(0, NCH // 2) as i:
                for u in range(2):
                    body(chunk_of(i, u))
            body(last_chunk)

        group_of = SLOTS

        def chunk4(i, n):
            return Chunk(group_of * i + n, CH, i, n)

        tail4 = Chunk(NCH, TAIL, NCH // group_of, 0)
        assert NCH % group_of == 0
        rows_in_of, rows_out_of = four("rows_in"), four("rows_out")

        def all_groups(eng, body, beside=None):
            for n in range(group_of):
                body(chunk4(0, n), True)
                if n == 1 and beside:
                    beside()
            with eng.Fori(0, NCH // group_of - 1) as i:
                for n in range(group_of):
                    body(chunk4(i + 1, n), False)
            body(tail4, False)

        with nc.Block() as block:
            @block.sync
            def _(sp):
                def store(k):
                    sp.wait_ge(s["rows_done"], k.c + 1)
                    sp.dma_start(chunk(xn_dram, k.c, k.n), rows_xn[k.u][0:k.rows, 0:k.tiles, :]).then_inc(rows_out_of[k.u], 16)

                for n in range(group_of):
                    sp.dma_start(rows_in[n], chunk(x, n)).then_inc(rows_in_of[n], 16)
                with sp.Fori(0, NCH // group_of - 1) as i:
                    for n in range(group_of):
                        store(chunk4(i, n))
                        sp.dma_start(rows_in[n], chunk(x, group_of * (i + 1) + n)).then_inc(rows_in_of[n], 16)
                last = NCH // group_of - 1
                store(chunk4(last, 0))
                sp.dma_start(rows_in[0][0:TAIL, 0:1, :], chunk(x, NCH, TAIL)).then_inc(rows_in_of[0], 16)
                for n in range(1, group_of):
                    store(chunk4(last, n))
                store(tail4)
                sp.wait_ge(rows_out_of[0], 16 * (last + 2))
                for n in range(1, group_of):
                    sp.wait_ge(rows_out_of[n], 16 * (last + 1))

            @block.scalar
            def _(act):
                for idx_in, a in zip(idx_i, (src, dst)):
                    act.wait_ge(s["const_pool"], 3)
                    act.dma_start(idx_in[0:NST, :], a[0:NST * ST].rearrange("(s e) -> s e", s=NST)).then_inc(s["tables_in"], 16)
                    act.dma_start(idx_in[NST:NBASE, 0:ETAIL * J], a[NST * ST:E].rearrange("(s e) -> s e", s=1)).then_inc(s["tables_in"], 16)
                act.dma_start(bases[0:1, 0:NBASE], bass.AP(dst.tensor, 0, [[1, 1], [ST, NBASE]])).then_inc(s["flag_in"], 16)
                for w_in, w in ((wk_in, mix["wk"]), (wv_in, mix["wv"]), (wo_in, mix["wo"]), (wq, mix["wq"])):
                    act.dma_start(w_in[:, :, :], w.rearrange("(k p) c -> p k c", p=P)).then_inc(s["weights_in"], 16)
                act.dma_start(rw_in, ffn["router_w"]).then_inc(s["weights_in"], 16)

                def weights():
                    act.wait_ge(s["weight_t"], 1)
                    for ki in range(KC):
                        ins = act.activation(wkvT[:, ki, :], ps[:, 4 + ki, :], ACT.Copy)
                    ins.then_inc(s["weight_done"], 1)
                    act.wait_ge(s["weight_t"], 2)
                    act.activation(woT[:, :, :], ps[:, 6, :].rearrange("p (k c) -> p k c", k=KC), ACT.Copy)
                    act.activation(v_rw, ps[:, 7, 0:KC * NE].rearrange("p (k e) -> p k e", k=KC), ACT.Copy).then_inc(s["weight_done"], 1)

                def copy_turned(k, first):
                    act.wait_ge(s["turned"], k.c + 1)
                    if not first:
                        act.sem_inc(s["carrier"], 1)
                    for to in (hT, xnT):
                        for kc in range(KC):
                            last = act.activation(to[:, kc, bass.ds(k.c * CH, k.n)], ps[:, 2 * (k.u % 2) + kc, 0:k.n], ACT.Copy)
                    last.then_inc(s["copied"], 1)

                all_groups(act, copy_turned, weights)

            @block.vector
            def _(dve):
                dve.memset(ones[:, :], 1.0)
                dve.memset(hT[:, :, N:AGG], 0.0).then_inc(s["const_done"], 1)

                def tables():
                    steps = Steps(dve, s["table_steps"])
                    dve.wait_ge(s["const_pool"], 3)
                    steps.run(dve.memset(centre[:, :], 0.0))
                    for half in range(P // HEAD):
                        d = slice(half * HEAD, (half + 1) * HEAD)
                        dve.memset(centre[d, d], -1.0 / HEAD)
                    steps.run(dve.memset(tiny[:, 0, :], 0.0))
                    dve.tensor_tensor(centre[:, :], centre[:, :], ident[:, :], ALU.add).then_inc(s["const_done"], 1)

                    dve.wait_ge(s["tables_in"], 64)
                    dve.tensor_copy(idx_f[0], idx_i[0])
                    steps.run(dve.tensor_copy(idx_f[1], idx_i[1]))
                    steps.run(dve.tensor_scalar(tiny[0:NBASE, 1, 0:1], idx_f[1][:, 0:1], 1.0, None, ALU.mult))
                    dve.tensor_scalar(idx_f[1], idx_f[1], tiny[0:NBASE, 1, 0:1], None, ALU.subtract).then_inc(s["table_f"], 1)
                    srcT_v = srcT.rearrange("p (s j) -> p j s", j=J)
                    rel_v = rel.rearrange("p (s j) -> p j s", j=J)
                    dve.memset(rel, -1.0)
                    steps.run(dve.memset(srcT.bitcast(I32), 0))
                    for k, table in enumerate((srcT_v, rel_v)):
                        for h in range(2):
                            dve.wait_ge(s["table_t"], 2 * k + h + 1)
                            part = ps[:, 4 + h, 0:J // 2 * NBASE].rearrange("p (j s) -> p j s", j=J // 2)
                            dve.tensor_copy(table[:, h * J // 2:(h + 1) * J // 2, 0:NBASE], part).then_inc(s["table_done"], 1)
                    dve.wait_ge(s["flag_in"], 16)
                    dve.tensor_copy(base_row, bases[0:1, 0:NBASE]).then_inc(s["base_f"], 1)
                    dve.wait_ge(s["base_t"], 1)
                    dve.tensor_copy(basebc[:, 0:NBASE], ps[:, 7, 2 * P:2 * P + NBASE])

                def normalise(pair, ks, first):
                    r, m = slice(0, ks[0].rows), len(ks) * ks[0].tiles
                    sts = st[:, :, :, :].rearrange("p a t s -> p (a t) s")
                    mean, rstd, var, tmp = (tiny[:, n:n + 2, :].rearrange("p a t -> p (a t)") for n in (2, 4, 10, 12))
                    steps = Steps(dve, s["dve_steps"], pair * STATS_STEPS)
                    for n, k in enumerate(ks):
                        dve.wait_ge(rows_in_of[k.u], 16 * (k.i + 1))
                        for j in range(k.tiles):
                            last = dve.bn_stats(sts[r, n * TILES + j, :], rows_in[k.u][r, j, :])
                    steps.run(last)
                    stats_steps(dve, steps, sts[r, 0:m, :], mean[r, 0:m], var[r, 0:m], tmp[r, 0:m], C, rstd[r, 0:m])
                    assert steps.n == STATS_STEPS
                    for n, k in enumerate(ks):
                        if not first:
                            dve.wait_ge(rows_out_of[k.u], 16 * k.i)
                            dve.wait_ge(s["turned"], k.c - group_of + 1)
                        for j in range(k.tiles):
                            a = n * TILES + j
                            last = dve.tensor_scalar(rows_xn[k.u][r, j, :], rows_in[k.u][r, j, :], mean[r, a:a + 1],
                                                     rstd[r, a:a + 1], ALU.subtract, ALU.mult)
                        last.then_inc(s["rows_done"], 1)

                normalise(0, [chunk4(0, 0), chunk4(0, 1)], True)
                tables()
                normalise(1, [chunk4(0, 2), chunk4(0, 3)], True)
                with dve.Fori(0, NCH // group_of - 1) as i:
                    for h in range(2):
                        normalise(2 * i + 2 + h, [chunk4(i + 1, 2 * h), chunk4(i + 1, 2 * h + 1)], False)
                normalise(NCH // 2, [tail4], False)

            @block.gpsimd
            def _(pool):
                pool.memset(ident[:, :], 0.0).then_inc(s["const_pool"], 1)
                pool.wait_ge(s["const_pool"], 1)
                pool.affine_select(out=ident[:, :], in_=ident[:, :], compare_op=ALU.not_equal, fill=1.0, base=0,
                                   pattern=[[-1, P]], channel_multiplier=1).then_inc(s["const_pool"], 1)
                pool.iota(iota[:, :], [[1, WIN]], base=0, channel_multiplier=0,
                          allow_small_or_imprecise_dtypes=True)
                pool.memset(ea[:, 0:2 * ST], 0.0).then_inc(s["const_pool"], 1)
                for v, a in ((v_b1, gnn["b1"]), (v_gamma, gnn["bn_gamma"]), (v_beta, gnn["bn_beta"]), (v_b2, gnn["b2"]),
                             (v_lnw, gnn["ln_w"]), (v_lnb, gnn["ln_b"]), (v_gnw, gnn["gn_w"]), (v_gnb, gnn["gn_b"]),
                             (v_gnms, gnn["gn_ms"])):
                    pool.dma_start(v, a.rearrange("(k p) -> p k", p=P)).then_inc(s["vectors_in"], 16)
                for half in range(P // HEAD):
                    for v, a in ((v_kg, mix["ln_k_g"]), (v_kb, mix["ln_k_b"])):
                        pool.dma_start(v[half * HEAD:(half + 1) * HEAD, :], a.rearrange("(d o) -> d o", o=1)).then_inc(s["vectors_in"], 16)
                pool.dma_start(v_eb1, ffn["b1"].rearrange("e (k p) -> p e k", p=P)).then_inc(s["vectors_in"], 16)
                pool.dma_start(bo_row[:, :], mix["bo"].partition_broadcast(P)).then_inc(s["vectors_in"], 16)
                for n, a in enumerate((mix["ln_v_g"], mix["ln_v_b"])):
                    for half in range(P // HEAD):
                        pool.dma_start(vrow[:, n, half * HEAD:(half + 1) * HEAD], a.partition_broadcast(P)).then_inc(s["vectors_in"], 16)


            @block.tensor
            def _(pe):
                def weights_and_tables():
                    pe.wait_ge(s["const_pool"], 2)
                    pe.wait_ge(s["const_done"], 2)
                    pe.wait_ge(s["weights_in"], 80)
                    for n, w_in in enumerate((wk_in, wv_in)):
                        for ki in range(KC):
                            for ko in range(KC):
                                ins = pe.matmul(ps[:, 4 + ki, n * C + ko * P:n * C + (ko + 1) * P],
                                                w_in[:, ko, ki * P:(ki + 1) * P], centre[:, :], start=True, stop=True)
                    ins.then_inc(s["weight_t"], 1)
                    for ki in range(KC):
                        for ko in range(KC):
                            pe.transpose(ps[:, 6, ki * C + ko * P:ki * C + (ko + 1) * P],
                                         wo_in[:, ko, ki * P:(ki + 1) * P], ident[:, :])
                    for ki in range(KC):
                        ins = pe.transpose(ps[:, 7, ki * NE:(ki + 1) * NE], rw_in[:, ki * P:(ki + 1) * P],
                                           ident[0:NE, 0:NE])
                    ins.then_inc(s["weight_t"], 1)

                    pe.wait_ge(s["weight_done"], 1)
                    pe.wait_ge(s["table_f"], 1)
                    for k in range(2):
                        for h in range(2):
                            if k == 1:
                                pe.wait_ge(s["table_done"], h + 1)
                            for jj in range(J // 2):
                                j = h * J // 2 + jj
                                ins = pe.transpose(ps[:, 4 + h, jj * NBASE:(jj + 1) * NBASE],
                                                   idx_f[k].rearrange("s (p j) -> s j p", j=J)[:, j, :],
                                                   ident[0:NBASE, 0:NBASE])
                            ins.then_inc(s["table_t"], 1)

                    pe.wait_ge(s["weight_done"], 2)
                    pe.wait_ge(s["base_f"], 1)
                    pe.matmul(ps[:, 7, 2 * P:2 * P + NBASE], ones[0:1, :], base_row, start=True, stop=True).then_inc(s["base_t"], 1)

                def turn(k, first):
                    if not (first and k.u < 2):
                        pe.wait_ge(s["copied"], k.c - 1)
                    pe.wait_ge(s["rows_done"], k.c + 1)
                    for kc in range(KC):
                        for t in range(k.tiles):
                            last = pe.transpose(ps[:, 2 * (k.u % 2) + kc, t * P:t * P + k.rows],
                                                rows_xn[k.u][0:k.rows, t, kc * P:(kc + 1) * P],
                                                ident[0:k.rows, 0:k.rows])
                    last.then_inc(s["turned"], 1)

                pe.wait_ge(s["const_pool"], 2)
                all_groups(pe, turn, weights_and_tables)

        e_in, gathered, cur_ready, summed, messages, used, windowed = map(
            four, ("e_in", "gathered", "cur", "summed", "relu", "used", "windowed"))
        raw_done = [s["raw_done"], s["raw_done1"]]
        group = TILES * 2 * NH
        mixm = wkvT[:, 0, :].rearrange("p (k c) -> p k c", k=KC)
        rmat = sq[:, :].rearrange("p (k c) -> p k c", k=KC)
        w1_sb = [w[:, :, :].rearrange("p k c -> p (k c)") for w in (wq, woT)]
        assert H == KC * C
        xrows = kvraw[:, 0:TILES * C].rearrange("p (t c) -> p t c", t=TILES)

        def supertile(q, u, parts=P):
            return Supertile(SLOTS * q + u, parts, q, u)

        first_tail, last_tail = supertile(ROUNDS, 0), supertile(ROUNDS, 1, ETAIL)

        def other(k):
            return (k.u - 2, k.q + 1) if k.u >= 2 else (k.u + 2, k.q)

        def node_chunk(c, n=CH):
            return Chunk(c, n)

        tail = node_chunk(NCH, TAIL)

        with nc.Block() as block:
            @block.sync
            def _(sp):
                def load_edges(k):
                    sp.wait_ge(summed[k.u], CREDIT + k.q)
                    rows = edge_attr[bass.ds(k.s * ST, (k.r.stop) * J), :]
                    sp.dma_start(e_ring[k.r, k.u, :, :], rows.rearrange("(p j) c -> p j c", j=J)).then_inc(e_in[k.u], 16)

                def load_rows(k):
                    sp.dma_start(xrows[0:k.rows, 0:k.tiles, :], chunk(x, k.c, k.n)).then_inc(s["x_in"], 16)

                def store_base(k):
                    sp.wait_ge(s["base_added"], CREDIT + k.c + 1)
                    sp.dma_start(chunk(base_dram, k.c, k.n), xrows[0:k.rows, 0:k.tiles, :]).then_inc(s["base_out"], 16)
                    sp.wait_ge(s["base_out"], 16 * (k.c + 1))

                with sp.Fori(0, NCH) as i:
                    for u in range(SLOTS):
                        load_edges(supertile(i, u))
                for u in range(SLOTS):
                    load_edges(supertile(NCH, u))
                sp.wait_ge(s["kv_done"], CREDIT + NCH + 1)
                load_rows(node_chunk(0))
                with sp.Fori(0, NCH - 1) as i:
                    for u in range(SLOTS):
                        load_edges(supertile(i + NCH + 1, u))
                    store_base(node_chunk(i))
                    load_rows(node_chunk(i + 1))
                load_edges(first_tail)
                load_edges(last_tail)
                sp.wait_ge(s["m_copied"], 1)
                for kc in range(KC):
                    sp.dma_start(w1_sb[kc], gnn["W1"][kc * P:(kc + 1) * P, :]).then_inc(s["w1_in"], 16)
                store_base(node_chunk(NCH - 1))
                load_rows(tail)
                store_base(tail)

            @block.gpsimd
            def _(pool):
                def gather(k):
                    pool.wait_ge(used[k.u], CREDIT + k.q)
                    pool.wait_ge(cur_ready[k.u], k.q + 1)
                    pool.sem_inc(s["carrier"], 1)
                    for j in range(J):
                        pool.indirect_dma_start(
                            out=g_ring[k.r, k.u, j, :], out_offset=None, in_=xn_dram,
                            in_offset=bass.IndirectOffsetOnAxis(ap=cur[k.r, k.u, j:j + 1], axis=0),
                        ).then_inc(gathered[k.u], 16)

                with pool.Fori(0, ROUNDS) as i:
                    for u in range(SLOTS):
                        gather(supertile(i, u))
                gather(first_tail)
                gather(last_tail)

            @block.scalar
            def _(act):
                def stage(sup, u):
                    act.activation(cur[:, u, :], srcT[:, bass.ds(sup * J, J)], ACT.Copy).then_inc(cur_ready[u], 1)

                def relu(k):
                    act.wait_ge(summed[k.u], CREDIT + k.q + 1)
                    m = g_ring[k.r, k.u, :, :]
                    act.activation(m, m, ACT.Relu).then_inc(messages[k.u], 1)

                def edges(k):
                    relu(k)
                    stage(k.s + SLOTS, k.u)

                def stage_rows(k, users, n):
                    act.wait_ge(users, CREDIT + n)
                    act.sem_inc(s["carrier"], 1)
                    act.activation(xc[:, :, 0:k.n], xnT[:, :, bass.ds(k.c * CH, k.n)], ACT.Copy).then_inc(s["xc_ready"], 1)

                def keys_values(k, t):
                    r = slice(0, k.rows)
                    act.wait_ge(s["proj_done"], CREDIT + TILES * k.c + t + 1)
                    if t == 0:
                        act.wait_ge(s["kv_done"], CREDIT + k.c)
                    act.activation(kvraw[r, t * 2 * C:(t + 1) * 2 * C], ps[r, 2 + t % 2, :], ACT.Copy)
                    act.wait_ge(s["ssq_done"], CREDIT + TILES * k.c + t)
                    act.activation(sq[r, :], ps[r, 2 + t % 2, :], ACT.Square).then_inc(raw_done[t % 2], 1)

                for u in range(SLOTS):
                    stage(u, u)
                with act.Fori(0, NCH) as i:
                    k = node_chunk(i)
                    stage_rows(k, s["proj_done"], TILES * i)
                    edges(supertile(i, 0))
                    edges(supertile(i, 1))
                    keys_values(k, 0)
                    keys_values(k, 1)
                    edges(supertile(i, 2))
                    keys_values(k, 2)
                    keys_values(k, 3)
                    edges(supertile(i, 3))
                stage_rows(tail, s["proj_done"], TILES * NCH)
                edges(supertile(NCH, 0))
                edges(supertile(NCH, 1))
                keys_values(tail, 0)
                edges(supertile(NCH, 2))
                edges(supertile(NCH, 3))
                act.wait_ge(s["r_done"], 1)
                act.activation(rmat, ps[:, 7, :].rearrange("p (k c) -> p k c", k=KC), ACT.Copy).then_inc(s["r_copied"], 1)
                with act.Fori(0, NCH - 1) as i:
                    stage_rows(node_chunk(i), s["mixed"], i)
                    for u in range(SLOTS):
                        edges(supertile(i + NCH + 1, u))
                stage_rows(node_chunk(NCH - 1), s["mixed"], NCH - 1)
                relu(first_tail)
                stage_rows(tail, s["mixed"], NCH)
                relu(last_tail)

            @block.vector
            def _(dve):
                def add_attributes(k):
                    dve.wait_ge(gathered[k.u], 16 * J * (k.q + 1))
                    dve.wait_ge(e_in[k.u], 16 * (k.q + 1))
                    m = g_ring[k.r, k.u, :, :]
                    dve.tensor_tensor(m, m, e_ring[k.r, k.u, :, :], ALU.add).then_inc(summed[k.u], 1)

                def one_hot(k):
                    slot, n = other(k)
                    dve.wait_ge(used[slot], CREDIT + n)
                    parts = k.r.stop
                    dve.tensor_tensor(hot[k.r, k.b, :, :],
                                      iota[k.r, :].unsqueeze(1).to_broadcast([parts, J, WIN]),
                                      rel[k.r, bass.ds(k.s * J, J)].unsqueeze(2).to_broadcast([parts, J, WIN]),
                                      ALU.is_equal).then_inc(s["hot_ready"], 1)

                def window(k):
                    col = dve.value_load(bases[0:1, bass.ds(k.s, 1)], min_val=0, max_val=N - 1)
                    dve.wait_ge(used[k.u], CREDIT + k.q + 1)
                    prev = (k.u - 1, k.q + 1) if k.u else (SLOTS - 1, k.q)
                    dve.wait_ge(windowed[prev[0]], CREDIT + prev[1])
                    to = hT[:, :, bass.ds(col, WIN)]
                    dve.tensor_tensor(to, to, ps[:, k.b, 0:KC * WIN].rearrange("p (k w) -> p k w", k=KC),
                                      ALU.add).then_inc(windowed[k.u], 1)

                def squares(k, t):
                    r = slice(0, k.rows)
                    dve.wait_ge(raw_done[t % 2], CREDIT + (TILES // 2) * k.c + t // 2 + 1)
                    dve.tensor_reduce(rs[r, 0, t * 2 * NH:(t + 1) * 2 * NH], sq[r, :].rearrange("p (g d) -> p g d", d=HEAD),
                                      AX.X, ALU.add).then_inc(s["ssq_done"], 1)

                def scale_keys_values(k):
                    r, n = slice(0, k.rows), k.tiles * 2 * NH
                    steps = Steps(dve, s["kv_steps"], k.c * (1 + RSQRT_STEPS))
                    dve.wait_ge(s["ssq_done"], CREDIT + TILES * k.c + k.tiles)
                    v, y, h = (rs[r, m, 0:n] for m in range(3))
                    steps.run(dve.tensor_scalar(v, v, 1.0 / HEAD, EPS, ALU.mult, ALU.add))
                    rsqrt_steps(dve, steps, v, y, h)
                    kv = kvraw[r, 0:n * HEAD].rearrange("p (g d) -> p g d", d=HEAD)
                    dve.tensor_tensor(kv, kv, y.unsqueeze(2).to_broadcast([k.rows, n, HEAD]), ALU.mult).then_inc(s["scaled"], 1)

                def add_base(k, n):
                    r = slice(0, k.rows)
                    dve.wait_ge(s["x_in"], 16 * (k.c + 1))
                    dve.wait_ge(s["mixed"], CREDIT + k.c + 1)
                    rows = xrows[r, 0:k.tiles, :]
                    step = Steps(dve, s["am_steps"], n)
                    step.run(dve.tensor_tensor(rows, rows, ps[r, 2:4, :].rearrange("p b (t c) -> p (b t) c", c=C)[:, 0:k.tiles, :], ALU.add))
                    dve.tensor_tensor(rows, rows, bo_row[r, :].unsqueeze(1).to_broadcast([k.rows, k.tiles, C]),
                                      ALU.add).then_inc(s["base_added"], 1)

                mixing = Steps(dve, s["am_steps"])

                def key_value_sums():
                    sv, k_bias, k_col = sq[:, 0:C], tiny[:, 6, 0:1], tiny[:, 7, 0:KC]
                    dve.wait_ge(s["kv_done"], CREDIT + NCH + 1)
                    dve.wait_ge(s["vectors_in"], VECTORS)
                    dve.tensor_scalar(sv, ps[:, 6, 0:C], v_kb, None, ALU.mult)
                    mixing.run(dve.tensor_scalar(k_bias, v_kb, float(N), None, ALU.mult))
                    for p in range(KC):
                        dve.scalar_tensor_tensor(amat[:, p, :], ps[:, 4 + p, 0:P], v_kg, sv[:, p * P:(p + 1) * P],
                                                 ALU.mult, ALU.add)
                        last = dve.scalar_tensor_tensor(k_col[:, p:p + 1], ps[:, 4 + p, P:P + 1], v_kg, k_bias,
                                                        ALU.mult, ALU.add)
                    mixing.run(last)
                    for p in range(KC):
                        last = dve.tensor_tensor(amat[:, p, :], amat[:, p, :], vrow[:, 0, :], ALU.mult)
                    mixing.run(last)
                    for p in range(KC):
                        last = dve.scalar_tensor_tensor(amat[:, p, :], vrow[:, 1, :], k_col[:, p:p + 1], amat[:, p, :],
                                                        ALU.mult, ALU.add)
                    mixing.run(last)
                    mixing.run(dve.tensor_scalar(amat[:, :, :], amat[:, :, :], 1.0 / N, None, ALU.mult))
                    for p in range(KC):
                        dve.memset(amat[0:HEAD, p, HEAD:P], 0.0)
                        last = dve.memset(amat[HEAD:P, p, 0:HEAD], 0.0)
                    last.then_inc(s["am_ready"], 1)

                def add_identity():
                    dve.wait_ge(s["m_done"], 1)
                    mixing.run(dve.tensor_copy(mixm, ps[:, 7, :].rearrange("p (k c) -> p k c", k=KC)))
                    for p in range(KC):
                        d = mixm[:, p, p * P:(p + 1) * P]
                        last = dve.tensor_tensor(d, d, ident[:, :], ALU.add)
                    last.then_inc(s["m_copied"], 1)

                for b in (4, 5, 6):
                    last = dve.memset(ps[:, b, :], 0.0)
                last.then_inc(s["kv_zero"], 1)

                steps = Steps(dve, s["flag_steps"])
                f = tiny[:, 8, :]
                steps.run(dve.memset(f, 0.0))
                full, part = rel[:, 0:NST * J], rel[0:ETAIL, NST * J:NBASE * J]
                dve.tensor_reduce(f[:, 0:1], full, AX.X, ALU.max)
                dve.tensor_reduce(f[:, 1:2], full, AX.X, ALU.min)
                dve.tensor_reduce(f[0:ETAIL, 2:3], part, AX.X, ALU.max)
                steps.run(dve.tensor_reduce(f[0:ETAIL, 3:4], part, AX.X, ALU.min))
                steps.run(dve.tensor_tensor(f[:, 0:1], f[:, 0:1], f[:, 2:3], ALU.max))
                steps.run(dve.tensor_tensor(f[:, 1:2], f[:, 1:2], f[:, 3:4], ALU.min))
                steps.run(dve.tensor_scalar(f[:, 0:1], f[:, 0:1], float(1 - WIN), None, ALU.add))
                steps.run(dve.tensor_scalar(f[:, 1:2], f[:, 1:2], -1.0, None, ALU.mult))
                dve.tensor_tensor(f[:, 0:1], f[:, 0:1], f[:, 1:2], ALU.max).then_inc(s["flag_f"], 1)
                dve.wait_ge(s["flag_t"], 1)
                steps.run(dve.tensor_reduce(tiny[0:1, 9, 0:1], ps[0:1, 7, 0:P], AX.X, ALU.max))
                dve.wait_ge(s["flag_in"], 16)
                dve.tensor_scalar(flag[0:1, 0:1], tiny[0:1, 9, 0:1], 0.0, None, ALU.is_gt).then_inc(s["flag_c"], 1)

                def edges(k):
                    add_attributes(k)
                    one_hot(k)

                edges(supertile(0, 0))
                with dve.Fori(0, NCH) as i:
                    k = node_chunk(i)
                    edges(supertile(i, 1))
                    window(supertile(i, 0))
                    edges(supertile(i, 2))
                    squares(k, 0)
                    squares(k, 1)
                    window(supertile(i, 1))
                    edges(supertile(i, 3))
                    squares(k, 2)
                    squares(k, 3)
                    window(supertile(i, 2))
                    scale_keys_values(k)
                    edges(supertile(i + 1, 0))
                    window(supertile(i, 3))
                edges(supertile(NCH, 1))
                window(supertile(NCH, 0))
                squares(tail, 0)
                scale_keys_values(tail)
                edges(supertile(NCH, 2))
                window(supertile(NCH, 1))
                key_value_sums()
                edges(supertile(NCH, 3))
                window(supertile(NCH, 2))
                edges(supertile(NCH + 1, 0))
                window(supertile(NCH, 3))
                add_identity()
                n = mixing.n
                with dve.Fori(0, NCH - 1) as i:
                    edges(supertile(i + NCH + 1, 1))
                    window(supertile(i + NCH + 1, 0))
                    edges(supertile(i + NCH + 1, 2))
                    add_base(node_chunk(i), n + i)
                    window(supertile(i + NCH + 1, 1))
                    edges(supertile(i + NCH + 1, 3))
                    window(supertile(i + NCH + 1, 2))
                    edges(supertile(i + NCH + 2, 0))
                    window(supertile(i + NCH + 1, 3))
                add_base(node_chunk(NCH - 1), n + NCH - 1)
                edges(last_tail)
                window(first_tail)
                add_base(tail, n + NCH)
                window(last_tail)
                dve.wait_ge(windowed[1], CREDIT + ROUNDS + 1)

            @block.tensor
            def _(pe):
                def sum_by_destination(k):
                    pe.wait_ge(messages[k.u], k.q + 1)
                    pe.wait_ge(s["hot_ready"], k.s + 1)
                    slot, n = other(k)
                    pe.wait_ge(windowed[slot], CREDIT + n)
                    for kc in range(KC):
                        for j in range(J):
                            last = pe.matmul(ps[:, k.b, kc * WIN:(kc + 1) * WIN], g_ring[k.r, k.u, j, kc * P:(kc + 1) * P],
                                             hot[k.r, k.b, j, :], start=(kc == 0 and j == 0), stop=(j == J - 1),
                                             skip_group_check=True)
                    last.then_inc(used[k.u], 1)

                def project(k, t):
                    if t == 0:
                        pe.wait_ge(s["xc_ready"], k.c + 1)
                    pe.wait_ge(raw_done[t % 2], CREDIT + (TILES // 2) * k.c + t // 2)
                    for kc in range(KC):
                        last = pe.matmul(ps[0:k.rows, 2 + t % 2, :], xc[:, kc, t * P:t * P + k.rows], wkvT[:, kc, :],
                                         start=(kc == 0), stop=(kc == KC - 1))
                    last.then_inc(s["proj_done"], 1)

                def sum_keys_values(k):
                    pe.wait_ge(s["scaled"], k.c + 1)
                    r = slice(0, k.rows)
                    flags = dict(start=False, stop=False, skip_group_check=True)
                    for t in range(k.tiles):
                        for p in range(KC):
                            keys = kvraw[r, t * 2 * C + p * P:t * 2 * C + (p + 1) * P]
                            values = kvraw[r, t * 2 * C + C + p * P:t * 2 * C + C + (p + 1) * P]
                            pe.matmul(ps[:, 4 + p, 0:P], keys, values, **flags)
                            pe.matmul(ps[:, 4 + p, P:P + 1], keys, ones[r, 0:1], **flags)
                            last = pe.matmul(ps[:, 6, p * P:(p + 1) * P], ones[r, :], values, **flags)
                    last.then_inc(s["kv_done"], 1)

                def mix_rows(k, n):
                    pe.wait_ge(s["xc_ready"], n)
                    pe.wait_ge(s["base_added"], CREDIT + k.c)
                    for t in range(k.tiles):
                        for kc in range(KC):
                            last = pe.matmul(ps[0:k.rows, 2 + t // 2, (t % 2) * C:(t % 2 + 1) * C],
                                             xc[:, kc, t * P:t * P + k.rows], mixm[:, kc, :],
                                             start=(kc == 0), stop=(kc == KC - 1), skip_group_check=True)
                    last.then_inc(s["mixed"], 1)

                for credited in (*summed, *used, *windowed, *raw_done, s["proj_done"], s["kv_done"], s["ssq_done"], s["mixed"],
                                 s["base_added"]):
                    pe.sem_inc(credited, CREDIT)
                pe.wait_ge(s["flag_f"], 1)
                pe.transpose(ps[0:1, 7, 0:P], tiny[:, 8, 0:1], ident[:, :]).then_inc(s["flag_t"], 1)
                pe.wait_ge(s["kv_zero"], 1)
                pe.wait_ge(s["flag_c"], 1)
                with pe.Fori(0, NCH) as i:
                    k = node_chunk(i)
                    sum_by_destination(supertile(i, 0))
                    project(k, 0)
                    project(k, 1)
                    sum_by_destination(supertile(i, 1))
                    project(k, 2)
                    project(k, 3)
                    sum_by_destination(supertile(i, 2))
                    sum_by_destination(supertile(i, 3))
                    sum_keys_values(k)
                sum_by_destination(supertile(NCH, 0))
                project(tail, 0)
                sum_by_destination(supertile(NCH, 1))
                sum_keys_values(tail)
                sum_by_destination(supertile(NCH, 2))
                pe.wait_ge(s["am_ready"], 1)
                for p in range(KC):
                    last = pe.matmul(ps[:, 7, p * C:(p + 1) * C], amat[:, p, :], wq[:, p, :], start=True, stop=True)
                last.then_inc(s["r_done"], 1)
                sum_by_destination(supertile(NCH, 3))
                pe.wait_ge(s["r_copied"], 1)
                for m in range(KC):
                    for p in range(KC):
                        last = pe.matmul(ps[:, 7, m * C:(m + 1) * C], rmat[:, p, m * P:(m + 1) * P], woT[:, p, :],
                                         start=(p == 0), stop=(p == KC - 1), skip_group_check=True)
                last.then_inc(s["m_done"], 1)
                pe.wait_ge(s["m_copied"], 1)
                with pe.Fori(0, NCH - 1) as i:
                    sum_by_destination(supertile(i + NCH + 1, 0))
                    mix_rows(node_chunk(i), NCH + 1 + i + 1)
                    for u in range(1, SLOTS):
                        sum_by_destination(supertile(i + NCH + 1, u))
                mix_rows(node_chunk(NCH - 1), 2 * NCH + 1)
                sum_by_destination(first_tail)
                mix_rows(tail, 2 * NCH + 2)
                sum_by_destination(last_tail)

        gsem = {n: sem("general_" + n) for n in
                                  ("e", "g", "cur", "sum", "msg", "rel", "hot", "used", "added", "steps")}
        gcur, grel, gmask = cur[:, 0, :], tiny[:, 10:12, :].rearrange("p a b -> p (a b)"), tiny[:, 12:14, :].rearrange("p a b -> p (a b)")

        def if_outside(eng, body):
            outside = eng.value_load(flag[0:1, 0:1], min_val=0, max_val=1)
            with eng.If(outside > 0):
                body()
            eng.sem_inc(s["carrier"], 1)

        def each_supertile(eng, body):
            with eng.Fori(0, NST) as i:
                body(Supertile(i))
            body(Supertile(NST, ETAIL))

        with nc.Block() as block:
            @block.sync
            def _(sp):
                def body():
                    def load(k):
                        sp.wait_ge(gsem["added"], CREDIT + NWIN * k.s)
                        rows = edge_attr[bass.ds(k.s * ST, k.r.stop * J), :]
                        sp.dma_start(e_ring[k.r, 0, :, :], rows.rearrange("(p j) c -> p j c", j=J)).then_inc(gsem["e"], 16)
                    each_supertile(sp, load)
                if_outside(sp, body)

            @block.gpsimd
            def _(pool):
                def body():
                    def gather(k):
                        pool.wait_ge(gsem["cur"], k.s + 1)
                        pool.sem_inc(s["carrier"], 1)
                        for j in range(J):
                            pool.indirect_dma_start(
                                out=g_ring[k.r, 0, j, :], out_offset=None, in_=xn_dram,
                                in_offset=bass.IndirectOffsetOnAxis(ap=gcur[k.r, j:j + 1], axis=0)).then_inc(gsem["g"], 16)
                    each_supertile(pool, gather)
                if_outside(pool, body)

            @block.scalar
            def _(act):
                def body():
                    def relu(k):
                        act.wait_ge(gsem["added"], CREDIT + NWIN * k.s)
                        act.sem_inc(s["carrier"], 1)
                        act.activation(gcur, srcT[:, bass.ds(k.s * J, J)], ACT.Copy).then_inc(gsem["cur"], 1)
                        act.wait_ge(gsem["sum"], k.s + 1)
                        m = g_ring[k.r, 0, :, :]
                        act.activation(m, m, ACT.Relu).then_inc(gsem["msg"], 1)
                    each_supertile(act, relu)
                if_outside(act, body)

            @block.vector
            def _(dve):
                def body():
                    def add(k):
                        dve.wait_ge(gsem["g"], 16 * J * (k.s + 1))
                        dve.wait_ge(gsem["e"], 16 * (k.s + 1))
                        m = g_ring[k.r, 0, :, :]
                        dve.tensor_tensor(m, m, e_ring[k.r, 0, :, :], ALU.add).then_inc(gsem["sum"], 1)
                        steps = Steps(dve, gsem["steps"], k.s * 5)
                        col = rel[:, bass.ds(k.s * J, J)]
                        base = basebc[:, bass.ds(k.s, 1)].to_broadcast([P, J])
                        dve.tensor_scalar(gmask, col, 0.0, None, ALU.is_lt)
                        steps.run(dve.tensor_scalar(grel, col, float(WIN), None, ALU.is_ge))
                        steps.run(dve.tensor_tensor(gmask, gmask, grel, ALU.add))
                        steps.run(dve.tensor_tensor(grel, col, base, ALU.add))
                        steps.run(dve.scalar_tensor_tensor(grel, grel, 1.0, gmask, ALU.add, ALU.mult))
                        steps.run(dve.tensor_scalar(grel, grel, -1.0, None, ALU.add))

                        def window(w):
                            n = NWIN * k.s + w
                            dve.wait_ge(gsem["used"], CREDIT + n)
                            parts = k.r.stop
                            h = hot[k.r, 0, :, :]
                            dve.tensor_tensor(h, iota[k.r, :].unsqueeze(1).to_broadcast([parts, J, WIN]),
                                              grel[k.r, :].unsqueeze(2).to_broadcast([parts, J, WIN]), ALU.is_equal).then_inc(gsem["hot"], 1)
                            dve.wait_ge(gsem["hot"], n + 1)
                            dve.tensor_scalar(grel, grel, float(-WIN), None, ALU.add).then_inc(gsem["rel"], 1)
                            dve.wait_ge(gsem["rel"], n + 1)
                            dve.wait_ge(gsem["used"], CREDIT + n + 1)
                            to = hT[:, :, bass.ds(w * WIN, WIN)]
                            dve.tensor_tensor(to, to, ps[:, 0, 0:KC * WIN].rearrange("p (k w) -> p k w", k=KC),
                                              ALU.add).then_inc(gsem["added"], 1)

                        dve.sem_inc(s["carrier"], 1)
                        with dve.Fori(0, NWIN) as w:
                            window(w)
                    each_supertile(dve, add)
                    dve.wait_ge(gsem["added"], CREDIT + NWIN * NBASE)
                if_outside(dve, body)

            @block.tensor
            def _(pe):
                def body():
                    pe.sem_inc(gsem["added"], CREDIT)
                    pe.sem_inc(gsem["used"], CREDIT)

                    def sum_by_destination(k):
                        pe.wait_ge(gsem["msg"], k.s + 1)
                        pe.sem_inc(s["carrier"], 1)
                        with pe.Fori(0, NWIN) as w:
                            n = NWIN * k.s + w
                            pe.wait_ge(gsem["added"], CREDIT + n)
                            pe.wait_ge(gsem["hot"], n + 1)
                            for kc in range(KC):
                                for j in range(J):
                                    last = pe.matmul(ps[:, 0, kc * WIN:(kc + 1) * WIN], g_ring[k.r, 0, j, kc * P:(kc + 1) * P],
                                                     hot[k.r, 0, j, :], start=(kc == 0 and j == 0),
                                                     stop=(j == J - 1), skip_group_check=True)
                            last.then_inc(gsem["used"], 1)
                    each_supertile(pe, sum_by_destination)
                if_outside(pe, body)

        h1T = big[:, :].rearrange("p (m n) -> p m n", m=KH)
        h2T = hT
        w2_sb = kvraw[:, 0:KH * C].rearrange("p (k m) -> p k m", k=KH)
        until_mlp.close()
        mlp_parts = ctx.enter_context(ExitStack())
        w1_hi, w1_lo, w2_hi, w2_lo, op_hi, op_lo = (mlp_parts.enter_context(nc.sbuf_tensor(name, shape, F32R)) for name, shape in (
            ("w1_hi", [P, KC, H]), ("w1_lo", [P, KC, H]), ("w2_hi", [P, KH, C]), ("w2_lo", [P, KH, C]),
            ("op_hi", [P, 2, KC * CH]), ("op_lo", [P, 2, KC * CH])))
        HF = KC * CH // KH
        assert CH == 2 * HF and TAIL <= HF

        def first_op(op, k):
            return op[:, k.u, :].rearrange("p (k n) -> p k n", k=KC)[:, :, 0:k.n]

        def second_op(op, h, n):
            return op[:, h, :].rearrange("p (k n) -> p k n", k=KH)[:, :, 0:n]

        def halves(k):
            return [(0, k.c * CH, HF), (1, k.c * CH + HF, HF)] if k.n == CH else [(0, k.c * CH, k.n)]

        def products(hi_a, lo_a, hi_b, lo_b):
            return ((hi_a, hi_b), (hi_a, lo_b), (lo_a, hi_b))

        eb2 = sq[0:NE, 0:C]
        bn1 = xc[:, 0, :]
        bn2 = xc[:, 1, :]
        NS = (NCH + 1) * 6
        coef = rs[:, :, :].rearrange("p a b -> p (a b)")
        scale1, shift1, tmp1, mv1 = coef[:, 0:KH], coef[:, KH:2 * KH], coef[:, 2 * KH:3 * KH], coef[:, 16:16 + 2 * KH]
        g = [coef[:, 32 + KC * n:32 + KC * (n + 1)] for n in range(14)]
        m = {n: sem("mlp_" + n) for n in
                               """w2 eb w_hi w_lo op_hi op_lo parts_hi parts_lo half_done relu ew_in0 ew_in1 ln1_0 ln1_1 copied0 copied1 stats0 stats1 scale steps 
                               copied2_0 copied2_1 added2_0 added2_1 mean1 sum_in""".split()}

        with nc.Block() as block:
            @block.sync
            def _(sp):
                sp.dma_start(w2_sb, gnn["W2"].rearrange("(k p) m -> p k m", p=P)).then_inc(m["w2"], 16)
                sp.dma_start(eb2, ffn["b2"]).then_inc(m["eb"], 16)
                sp.wait_ge(m["eb"], 16)

            @block.tensor
            def _(pe):
                def first(k):
                    pe.wait_ge((m["copied0"], m["copied1"])[k.u], CREDIT + k.i)
                    pe.wait_ge(m["op_lo"], k.c + 1)
                    hi, lo = first_op(op_hi, k), first_op(op_lo, k)
                    for mt in range(KH):
                        c = slice(mt * P, (mt + 1) * P)
                        terms = [(w[:, kc, c], x[:, kc, :]) for kc in range(KC) for w, x in products(w1_hi, w1_lo, hi, lo)]
                        for n, (w, x) in enumerate(terms):
                            last = pe.matmul(ps[:, 4 * k.u + mt, 0:k.n], w, x, start=(n == 0), stop=(n == len(terms) - 1))
                    last.then_inc((m["ln1_0"], m["ln1_1"])[k.u], 1)

                def second(k):
                    pe.wait_ge((m["copied2_0"], m["copied2_1"])[k.u], CREDIT + k.i)
                    pe.wait_ge((m["added2_0"], m["added2_1"])[k.u], CREDIT + k.i)
                    for h, _, nodes in halves(k):
                        pe.wait_ge(m["parts_lo"], 2 * k.c + h + 1)
                        hi, lo = second_op(op_hi, h, nodes), second_op(op_lo, h, nodes)
                        for mt in range(KC):
                            c = slice(mt * P, (mt + 1) * P)
                            terms = [(w[:, kh, c], x[:, kh, :]) for kh in range(KH) for w, x in products(w2_hi, w2_lo, hi, lo)]
                            for n, (w, x) in enumerate(terms):
                                last = pe.matmul(ps[:, 2 * k.u + mt, h * HF:h * HF + nodes], w, x, start=(n == 0),
                                                 stop=(n == len(terms) - 1), skip_group_check=True)
                        last.then_inc(m["half_done"], 1)

                for credited in (m["copied0"], m["copied1"], m["copied2_0"], m["copied2_1"], m["added2_0"], m["added2_1"], m["half_done"]):
                    pe.sem_inc(credited, CREDIT)
                pe.wait_ge(m["w_lo"], KC)
                all_chunks(pe, first)
                pe.wait_ge(m["w_lo"], KC + 1)
                all_chunks(pe, second)
                pe.wait_ge(m["sum_in"], 1)
                pe.matmul(ps[:, 6, 0:KC], ones[:, :], g[0], start=True, stop=True).then_inc(m["mean1"], 1)
                pe.wait_ge(m["sum_in"], 2)
                pe.matmul(ps[:, 7, 0:KC], ones[:, :], g[3], start=True, stop=True).then_inc(m["mean1"], 1)

            @block.scalar
            def _(act):
                def split(k):
                    act.activation(first_op(op_hi, k), hT[:, :, bass.ds(k.c * CH, k.n)], ACT.Copy).then_inc(m["op_hi"], 1)

                def first(k, nxt):
                    act.wait_ge((m["ln1_0"], m["ln1_1"])[k.u], k.i + 1)
                    act.sem_inc(s["carrier"], 1)
                    if nxt:
                        split(nxt)
                    for mt in range(KH):
                        last = act.activation(h1T[:, mt, bass.ds(k.c * CH, k.n)], ps[:, 4 * k.u + mt, 0:k.n], ACT.Identity,
                                              bias=v_b1[:, mt:mt + 1])
                    last.then_inc((m["copied0"], m["copied1"])[k.u], 1)

                def relu(k, tiles=range(KH)):
                    for mt in tiles:
                        a = h1T[:, mt, bass.ds(k.c * CH, k.n)]
                        last = act.activation(a, a, ACT.Relu, bias=shift1[:, mt:mt + 1], scale=scale1[:, mt:mt + 1])
                    if mt == KH - 1:
                        last.then_inc(m["relu"], 1)

                def high_halves(k, first_chunk=False, between=None):
                    act.wait_ge(m["relu"], k.c + 1)
                    for h, node, nodes in halves(k):
                        if h == 1 and between:
                            between()
                        if not first_chunk:
                            act.wait_ge(m["half_done"], CREDIT + 2 * k.c + h - 1)
                        act.sem_inc(s["carrier"], 1)
                        act.activation(second_op(op_hi, h, nodes), h1T[:, :, bass.ds(node, nodes)], ACT.Copy).then_inc(m["parts_hi"], 1)

                def second(k):
                    act.wait_ge(m["half_done"], CREDIT + 2 * k.c + len(halves(k)))
                    act.sem_inc(s["carrier"], 1)
                    act.activation(h2T[:, 0, bass.ds(k.c * CH, k.n)], ps[:, 2 * k.u, 0:k.n], ACT.Identity,
                                   bias=v_b2[:, 0:1]).then_inc((m["copied2_0"], m["copied2_1"])[k.u], 1)

                act.wait_ge(s["w1_in"], 16 * KC)
                for kc in range(KC):
                    act.activation(w1_hi[:, kc, :], w1_sb[kc], ACT.Copy).then_inc(m["w_hi"], 1)
                split(chunk_of(0, 0))
                split(chunk_of(0, 1))
                act.wait_ge(m["w2"], 16)
                act.activation(w2_hi[:, :, :], w2_sb, ACT.Copy).then_inc(m["w_hi"], 1)
                with act.Fori(0, NCH // 2 - 1) as i:
                    for u in range(2):
                        first(chunk_of(i, u), chunk_of(i + 1, u))
                first(chunk_of(NCH // 2 - 1, 0), last_chunk)
                first(chunk_of(NCH // 2 - 1, 1), None)
                first(last_chunk, None)
                act.wait_ge(m["scale"], 1)
                relu(chunk_of(0, 0))
                high_halves(chunk_of(0, 0), True)
                relu(chunk_of(0, 1))
                with act.Fori(0, NCH // 2 - 1) as i:
                    for k, nxt, after in ((chunk_of(i, 0), chunk_of(i, 1), chunk_of(i + 1, 0)),
                                          (chunk_of(i, 1), chunk_of(i + 1, 0), chunk_of(i + 1, 1))):
                        high_halves(nxt, between=lambda: relu(after, range(KH // 2)))
                        second(k)
                        relu(after, range(KH // 2, KH))
                high_halves(chunk_of(NCH // 2 - 1, 1))
                second(chunk_of(NCH // 2 - 1, 0))
                relu(last_chunk)
                high_halves(last_chunk)
                second(chunk_of(NCH // 2 - 1, 1))
                second(last_chunk)
                act.activation(tiny[:, 15, 0:1], ident[:, 0:1], ACT.Gelu)

            @block.vector
            def _(dve):
                def stats(k, a, bn, tiles, copied, done):
                    dve.wait_ge(copied[k.u], CREDIT + k.i + 1)
                    for mt in range(tiles):
                        last = dve.bn_stats(bn[:, bass.ds(k.c * 6 + mt * NS, 6)], a[:, mt, bass.ds(k.c * CH, k.n)])
                    last.then_inc(done, 1)

                def split(k):
                    dve.wait_ge(m["op_hi"], k.c + 1)
                    dve.tensor_tensor(first_op(op_lo, k), hT[:, :, bass.ds(k.c * CH, k.n)], first_op(op_hi, k).bitcast(F32),
                                      ALU.subtract).then_inc(m["op_lo"], 1)

                def first(k, nxt):
                    if nxt:
                        split(nxt)
                    stats(k, h1T, bn1, KH, (m["copied0"], m["copied1"]), m["stats0"])

                def low_halves(k):
                    for h, node, nodes in halves(k):
                        dve.wait_ge(m["parts_hi"], 2 * k.c + h + 1)
                        dve.tensor_tensor(second_op(op_lo, h, nodes), h1T[:, :, bass.ds(node, nodes)],
                                          second_op(op_hi, h, nodes).bitcast(F32), ALU.subtract).then_inc(m["parts_lo"], 1)

                def second_stats(k):
                    dve.wait_ge(m["half_done"], CREDIT + 2 * k.c + len(halves(k)))
                    for mt in range(1, KC):
                        last = dve.tensor_scalar(h2T[:, mt, bass.ds(k.c * CH, k.n)], ps[:, 2 * k.u + mt, 0:k.n],
                                                 v_b2[:, mt:mt + 1], None, ALU.add)
                    last.then_inc((m["added2_0"], m["added2_1"])[k.u], 1)
                    dve.wait_ge((m["added2_0"], m["added2_1"])[k.u], CREDIT + k.i + 1)
                    stats(k, h2T, bn2, KC, (m["copied2_0"], m["copied2_1"]), m["stats1"])

                for kc in range(KC):
                    dve.wait_ge(m["w_hi"], kc + 1)
                    dve.tensor_tensor(w1_lo[:, kc, :], w1_sb[kc], w1_hi[:, kc, :].bitcast(F32), ALU.subtract).then_inc(m["w_lo"], 1)
                split(chunk_of(0, 0))
                split(chunk_of(0, 1))
                dve.wait_ge(m["w_hi"], KC + 1)
                dve.tensor_tensor(w2_lo[:, :, :], w2_sb, w2_hi[:, :, :].bitcast(F32), ALU.subtract).then_inc(m["w_lo"], 1)
                with dve.Fori(0, NCH // 2 - 1) as i:
                    for u in range(2):
                        first(chunk_of(i, u), chunk_of(i + 1, u))
                first(chunk_of(NCH // 2 - 1, 0), last_chunk)
                first(chunk_of(NCH // 2 - 1, 1), None)
                first(last_chunk, None)
                dve.wait_ge(m["stats0"], NCH + 1)
                steps = Steps(dve, m["steps"])
                for mt in range(KH):
                    last = dve.bn_aggr(mv1[:, 2 * mt:2 * mt + 2], bn1[:, mt * NS:(mt + 1) * NS])
                steps.run(last)
                mean, var = (mv1.rearrange("p (m a) -> p m a", a=2)[:, :, a] for a in range(2))
                steps.run(dve.tensor_scalar(shift1, var, EPS, None, ALU.add))
                rsqrt_steps(dve, steps, shift1, scale1, tmp1)
                steps.run(dve.tensor_tensor(scale1, scale1, v_gamma, ALU.mult))
                steps.run(dve.tensor_tensor(tmp1, scale1, mean, ALU.mult))
                dve.tensor_tensor(shift1, v_beta, tmp1, ALU.subtract).then_inc(m["scale"], 1)

                low_halves(chunk_of(0, 0))
                with dve.Fori(0, NCH // 2 - 1) as i:
                    low_halves(chunk_of(i, 1))
                    second_stats(chunk_of(i, 0))
                    low_halves(chunk_of(i + 1, 0))
                    second_stats(chunk_of(i, 1))
                low_halves(chunk_of(NCH // 2 - 1, 1))
                second_stats(chunk_of(NCH // 2 - 1, 0))
                low_halves(last_chunk)
                second_stats(chunk_of(NCH // 2 - 1, 1))
                second_stats(last_chunk)
                dve.wait_ge(m["stats1"], NCH + 1)
                mv2 = coef[:, 16 + 2 * KH:16 + 2 * KH + 2 * KC]
                for mt in range(KC):
                    last = dve.bn_aggr(mv2[:, 2 * mt:2 * mt + 2], bn2[:, mt * NS:(mt + 1) * NS])
                steps.run(last)
                mean, var = (mv2.rearrange("p (m a) -> p m a", a=2)[:, :, a] for a in range(2))
                dve.tensor_copy(g[0], mean).then_inc(m["sum_in"], 1)
                dve.wait_ge(m["mean1"], 1)
                steps.run(dve.tensor_copy(g[1], ps[:, 6, 0:KC]))
                steps.run(dve.tensor_reduce(g[2][:, 0:1], g[1], AX.X, ALU.add))
                steps.run(dve.tensor_scalar(g[2][:, 0:1], g[2][:, 0:1], 1.0 / C, None, ALU.mult))
                mean_g = g[2][:, 0:1]
                steps.run(dve.tensor_scalar(g[1], mean, mean_g, None, ALU.subtract))
                steps.run(dve.tensor_tensor(g[3], g[1], g[1], ALU.mult))
                dve.tensor_tensor(g[3], g[3], var, ALU.add).then_inc(m["sum_in"], 1)
                dve.wait_ge(m["mean1"], 2)
                steps.run(dve.tensor_copy(g[4], ps[:, 7, 0:KC]))
                steps.run(dve.tensor_reduce(g[5][:, 0:1], g[4], AX.X, ALU.add))
                steps.run(dve.tensor_scalar(g[5][:, 0:1], g[5][:, 0:1], 1.0 / C, EPS, ALU.mult, ALU.add))
                rsqrt_steps(dve, steps, g[5][:, 0:1], g[6][:, 0:1], g[6][:, 1:2])
                a1, b1, m1, v1 = g[7], g[8], g[9], g[10]
                steps.run(dve.tensor_scalar(a1, v_lnw, g[6][:, 0:1], None, ALU.mult))
                steps.run(dve.tensor_tensor(m1, g[1], a1, ALU.mult))
                steps.run(dve.tensor_tensor(m1, m1, v_lnb, ALU.add))
                steps.run(dve.tensor_scalar(b1, a1, mean_g, None, ALU.mult))
                steps.run(dve.tensor_tensor(b1, v_lnb, b1, ALU.subtract))
                steps.run(dve.tensor_tensor(v1, a1, a1, ALU.mult))
                steps.run(dve.tensor_tensor(v1, v1, var, ALU.mult))
                steps.run(dve.tensor_tensor(g[11], m1, v_gnms, ALU.mult))
                steps.run(dve.tensor_tensor(g[12], m1, g[11], ALU.subtract))
                steps.run(dve.tensor_tensor(g[12], g[12], g[12], ALU.mult))
                steps.run(dve.tensor_tensor(v1, v1, g[12], ALU.add))
                steps.run(dve.tensor_scalar(v1, v1, EPS, None, ALU.add))
                rsqrt_steps(dve, steps, v1, g[12], g[13])
                steps.run(dve.tensor_tensor(g[12], g[12], v_gnw, ALU.mult))
                steps.run(dve.tensor_tensor(g[11], b1, g[11], ALU.subtract))
                steps.run(dve.tensor_tensor(g[11], g[11], g[12], ALU.mult))
                steps.run(dve.tensor_tensor(shift1[:, 0:KC], g[11], v_gnb, ALU.add))
                steps.run(dve.tensor_tensor(scale1[:, 0:KC], a1, g[12], ALU.mult))

        mlp_parts.close()
        until_ffn.close()
        scratch = sb("scratch", [P, SLOTS * J * C])
        off = [0]

        def load_expert(sp, e):
            for n, w in enumerate((ffn["w1"], ffn["w2"])):
                sp.dma_start(ew_in[:, e % 2, n, :, :], w[e].rearrange("(k p) m -> p k m", p=P)).then_inc((m["ew_in0"], m["ew_in1"])[e % 2], 16)

        def part(n):
            off[0] += n
            assert off[0] <= SLOTS * J * C + KC * 2 * C
            place = scratch if off[0] <= SLOTS * J * C else wkvT[:, :, :].rearrange("p k c -> p (k c)")
            at = off[0] - (0 if off[0] <= SLOTS * J * C else SLOTS * J * C)
            return place[:, at - n:at]

        ew_in = part(2 * 2 * KC * C).rearrange("p (s n k m) -> p s n k m", s=2, n=2, k=KC)
        gnnT = part(KC * CH).rearrange("p (k n) -> p k n", k=KC)
        base_in = [part(TILES * C).rearrange("p (t c) -> p t c", t=TILES) for _ in range(2)]
        tok = part(TILES * C).rearrange("p (t c) -> p t c", t=TILES)
        acc = [part(TILES * C).rearrange("p (t c) -> p t c", t=TILES) for _ in range(2)]
        comb = [part(TILES * NE).rearrange("p (t e) -> p t e", t=TILES) for _ in range(2)]
        combT = part(CH)[0:NE, :]
        logit, top, top_f, pick = (part(TILES * NE).rearrange("p (t e) -> p t e", t=TILES) for _ in range(4))
        top_i = part(TILES * NE).bitcast(U32).rearrange("p (t e) -> p t e", t=TILES)
        order = part(NE)
        tokT = xc
        hidT = [kvraw[:, n * KC * CH:(n + 1) * KC * CH].rearrange("p (k n) -> p k n", k=KC) for n in range(2)]
        tok_hi, tok_lo, hid_hi, hid_lo = ([sb(f"{name}{u}", [P, KC, CH], F32R) for u in range(2)]
                                          for name in ("tok_hi", "tok_lo", "hid_hi", "hid_lo"))
        ew1_hi, ew1_lo, ew2_hi, ew2_lo = (sb(name, [P, NE, KC, C], F32R) for name in ("ew1_hi", "ew1_lo", "ew2_hi", "ew2_lo"))

        f = {n: sem("ffn_" + n) for n in
                               """base0 base1 relu turned x1 normed steps tok_turned tok_copied routed top_ready share
                               combined comb_turned comb_copied b2_done acc_ready l1 hidden l2 added out0 out1 stored0 stored1 iota tok_lo hid_lo w_hi w_split""".split()}
        PREP_STEPS = 2 + (STATS_STEPS - 1) + 4 + 2

        with nc.Block() as block:
            @block.sync
            def _(sp):
                def load(k):
                    sp.wait_ge(f["x1"], k.c - 1)
                    sp.dma_start(base_in[k.u][0:k.rows, 0:k.tiles, :], chunk(base_dram, k.c, k.n)).then_inc((f["base0"], f["base1"])[k.u], 16)

                def store(k):
                    sp.wait_ge(f["added"], CREDIT + NE * (k.c + 1))
                    sp.dma_start(chunk(out, k.c, k.n), acc[k.u][0:k.rows, 0:k.tiles, :]).then_inc((f["out0"], f["out1"])[k.u], 16)

                for u in range(2):
                    sp.dma_start(base_in[u], chunk(base_dram, u)).then_inc((f["base0"], f["base1"])[u], 16)
                for e in range(NE):
                    if e >= 2:
                        sp.wait_ge(f["w_split"], 2 * (e - 1))
                    load_expert(sp, e)
                with sp.Fori(0, NCH // 2 - 1) as i:
                    for u in range(2):
                        load(chunk_of(i + 1, u))
                        store(chunk_of(i, u))
                        sp.wait_ge((f["out0"], f["out1"])[u], 16 * (i + 1))
                        sp.sem_inc((f["stored0"], f["stored1"])[u], 1)
                load(last_chunk)
                store(chunk_of(NCH // 2 - 1, 0))
                sp.wait_ge(f["out0"], 16 * (NCH // 2))
                sp.sem_inc(f["stored0"], 1)
                store(chunk_of(NCH // 2 - 1, 1))
                store(last_chunk)
                sp.wait_ge(f["out0"], 16 * (NCH // 2 + 1))
                sp.wait_ge(f["out1"], 16 * (NCH // 2))

            @block.gpsimd
            def _(pool):
                pool.iota(order, [[1, NE]], base=0, channel_multiplier=0,
                          allow_small_or_imprecise_dtypes=True).then_inc(f["iota"], 1)
                for e in range(NE):
                    for n, (hi, lo) in enumerate(((ew1_hi, ew1_lo), (ew2_hi, ew2_lo))):
                        w = ew_in[:, e % 2, n]
                        pool.wait_ge((m["ew_in0"], m["ew_in1"])[e % 2], 32 * (e // 2 + 1))
                        pool.tensor_copy(hi[:, e], w).then_inc(f["w_hi"], 1)
                        pool.wait_ge(f["w_hi"], 2 * e + n + 1)
                        pool.tensor_tensor(lo[:, e], w, hi[:, e].bitcast(F32), ALU.subtract).then_inc(f["w_split"], 1)

            def with_next(eng, body):
                with eng.Fori(0, NCH // 2 - 1) as i:
                    body(chunk_of(i, 0), chunk_of(i, 1))
                    body(chunk_of(i, 1), chunk_of(i + 1, 0))
                h = NCH // 2 - 1
                body(chunk_of(h, 0), chunk_of(h, 1))
                body(chunk_of(h, 1), last_chunk)
                body(last_chunk, None)

            @block.scalar
            def _(act):
                def relu(k):
                    act.wait_ge(f["turned"], CREDIT + k.c)
                    act.sem_inc(s["carrier"], 1)
                    for kc in range(KC):
                        last = act.activation(gnnT[:, kc, 0:k.n], h2T[:, kc, bass.ds(k.c * CH, k.n)], ACT.Relu,
                                              bias=shift1[:, kc:kc + 1], scale=scale1[:, kc:kc + 1])
                    last.then_inc(f["relu"], 1)

                def copy_tokens(k):
                    act.wait_ge(f["tok_turned"], CREDIT + k.c + 1)
                    for kc in range(KC):
                        act.activation(tokT[:, kc, 0:k.n], ps[:, kc, 0:k.n], ACT.Copy)
                        last = act.activation(tok_hi[k.u][:, kc, 0:k.n], ps[:, kc, 0:k.n], ACT.Copy)
                    last.then_inc(f["tok_copied"], 1)

                def share(k):
                    act.wait_ge(f["top_ready"], k.c + 1)
                    a = tiny[0:k.rows, 6, 0:k.tiles]
                    act.activation(a, a, ACT.Tanh, scale=0.5).then_inc(f["share"], 1)

                def copy_comb(k):
                    act.wait_ge(f["comb_turned"], k.c + 1)
                    act.activation(combT[:, 0:k.n], ps[0:NE, 2, 0:k.n], ACT.Copy).then_inc(f["comb_copied"], 1)

                def expert(k, e):
                    for mt in range(KC):
                        act.wait_ge(f["l1"], 2 * NE * k.c + 2 * e + mt + 1)
                        if mt == 0:
                            act.wait_ge(f["l2"], CREDIT + NE * k.c + max(e - 1, 0))
                        for hidden in (hidT[e % 2], hid_hi[e % 2]):
                            last = act.activation(hidden[:, mt, 0:k.n], ps[:, 3 + mt, 0:k.n], ACT.Gelu, bias=v_eb1[:, e, mt:mt + 1])
                        last.then_inc(f["hidden"], 1)

                def body(k, nxt):
                    if nxt:
                        relu(nxt)
                    for e in range(NE):
                        expert(k, e)
                        if nxt and e == 4:
                            copy_tokens(nxt)
                        if nxt and e == 6:
                            share(nxt)
                        if nxt and e == 7:
                            copy_comb(nxt)

                k = chunk_of(0, 0)
                relu(k), copy_tokens(k), share(k), copy_comb(k)
                with_next(act, body)

            @block.vector
            def _(dve):
                def steps_of(k, n):
                    steps = Steps(dve, f["steps"], k.c * PREP_STEPS)
                    steps.n = n
                    return steps

                def x1(k):
                    r, t = slice(0, k.rows), slice(0, k.tiles)
                    steps = steps_of(k, 0)
                    dve.wait_ge((f["base0"], f["base1"])[k.u], 16 * (k.i + 1))
                    dve.wait_ge(f["turned"], CREDIT + k.c + 1)
                    b = base_in[k.u][r, t, :]
                    steps.run(dve.tensor_tensor(b, b, ps[r, 0:2, :].rearrange("p b (t c) -> p (b t) c", c=C)[:, t, :], ALU.add))
                    for j in range(k.tiles):
                        last = dve.bn_stats(st[r, 0, j, :], base_in[k.u][r, j, :])
                    steps.run(last)
                    return steps.n

                def norm_stats(k, n):
                    r, t = slice(0, k.rows), slice(0, k.tiles)
                    steps = steps_of(k, n)
                    stats_steps(dve, steps, st[r, 0, t, :], tiny[r, 2, t], tiny[r, 4, t], tiny[r, 5, t], C, tiny[r, 3, t])
                    return steps.n

                def tokens(k, n):
                    r, t = slice(0, k.rows), slice(0, k.tiles)
                    steps = steps_of(k, n)
                    dve.wait_ge(f["tok_turned"], CREDIT + k.c)
                    for j in range(k.tiles):
                        last = dve.tensor_scalar(tok[r, j, :], base_in[k.u][r, j, :], tiny[r, 2, j:j + 1], tiny[r, 3, j:j + 1],
                                                 ALU.subtract, ALU.mult)
                    last.then_inc(f["normed"], 1)
                    dve.wait_ge(f["normed"], k.c + 1)
                    dve.wait_ge((f["stored0"], f["stored1"])[k.u], CREDIT + k.i)
                    dve.tensor_tensor(acc[k.u][r, t, :], base_in[k.u][r, t, :], tok[r, t, :], ALU.add).then_inc(f["x1"], 1)
                    return steps.n

                def choose(k, n):
                    r, t = slice(0, k.rows), slice(0, k.tiles)
                    steps = steps_of(k, n)
                    dve.wait_ge(f["routed"], k.c + 1)
                    steps.run(dve.tensor_copy(logit[r, t, :], ps[r, 2, 0:k.tiles * NE].rearrange("p (t e) -> p t e", e=NE)))
                    dve.sem_inc(s["carrier"], 1)
                    for j in range(k.tiles):
                        last = dve.max(top[r, j, :], logit[r, j, :])
                    steps.run(last)
                    dve.sem_inc(s["carrier"], 1)
                    for j in range(k.tiles):
                        last = dve.max_index(top_i[r, j, :], top[r, j, :], logit[r, j, :])
                    steps.run(last)
                    dve.tensor_tensor(tiny[r, 6, t], top[r, t, 0], top[r, t, 1], ALU.subtract).then_inc(f["top_ready"], 1)
                    steps.run(dve.tensor_copy(top_f[r, t, 0:2], top_i[r, t, 0:2]))
                    return steps.n

                def combine(k, n):
                    r, t = slice(0, k.rows), slice(0, k.tiles)
                    steps = steps_of(k, n)
                    shape = [k.rows, k.tiles, NE]
                    dve.wait_ge(f["share"], k.c + 1)
                    th, w0, w1 = tiny[r, 6, t], tiny[r, 7, t], tiny[r, 8, t]
                    dve.tensor_scalar(w0, th, 0.5, 0.5, ALU.mult, ALU.add)
                    dve.tensor_scalar(w1, th, -0.5, 0.5, ALU.mult, ALU.add)
                    dve.tensor_tensor(pick[r, t, :], order[r, :].unsqueeze(1).to_broadcast(shape),
                                      top_f[r, t, 1:2].to_broadcast(shape), ALU.is_equal)
                    steps.run(dve.tensor_tensor(comb[k.u][r, t, :], order[r, :].unsqueeze(1).to_broadcast(shape),
                                                top_f[r, t, 0:1].to_broadcast(shape), ALU.is_equal))
                    dve.tensor_tensor(pick[r, t, :], pick[r, t, :], w1.unsqueeze(2).to_broadcast(shape), ALU.mult)
                    steps.run(dve.tensor_tensor(comb[k.u][r, t, :], comb[k.u][r, t, :], w0.unsqueeze(2).to_broadcast(shape), ALU.mult))
                    dve.tensor_tensor(comb[k.u][r, t, :], comb[k.u][r, t, :], pick[r, t, :], ALU.add).then_inc(f["combined"], 1)
                    return steps.n

                def add_bias(k, n):
                    r, t = slice(0, k.rows), slice(0, k.tiles)
                    dve.wait_ge(f["b2_done"], k.c + 1)
                    a = acc[k.u][r, t, :]
                    dve.tensor_tensor(a, a, ps[r, 0:2, :].rearrange("p b (t c) -> p (b t) c", c=C)[:, t, :], ALU.add).then_inc(f["acc_ready"], 1)
                    assert n == PREP_STEPS, n

                def low_tokens(k):
                    dve.wait_ge(f["tok_copied"], k.c + 1)
                    dve.tensor_tensor(tok_lo[k.u][:, :, 0:k.n], tokT[:, :, 0:k.n], tok_hi[k.u][:, :, 0:k.n].bitcast(F32),
                                      ALU.subtract).then_inc(f["tok_lo"], 1)

                def low_hidden(k, e):
                    for mt in range(KC):
                        dve.wait_ge(f["hidden"], 2 * NE * k.c + 2 * e + mt + 1)
                        dve.tensor_tensor(hid_lo[e % 2][:, mt, 0:k.n], hidT[e % 2][:, mt, 0:k.n], hid_hi[e % 2][:, mt, 0:k.n].bitcast(F32),
                                          ALU.subtract).then_inc(f["hid_lo"], 1)

                def expert(k, e):
                    r = slice(0, k.rows)
                    dve.wait_ge(f["l2"], CREDIT + NE * k.c + e + 1)
                    dve.wait_ge(f["added"], CREDIT + NE * k.c + e)
                    if e == 0:
                        dve.wait_ge(f["acc_ready"], CREDIT + k.c + 1)
                    for j in range(k.tiles):
                        a = acc[k.u][r, j, :]
                        last = dve.scalar_tensor_tensor(a, ps[r, 5 + j // 2, (j % 2) * C:(j % 2 + 1) * C], comb[k.u][r, j, e:e + 1], a,
                                                        ALU.mult, ALU.add)
                    last.then_inc(f["added"], 1)

                def body(k, nxt):
                    n = 0
                    low_hidden(k, 0)
                    for e in range(NE):
                        if e + 1 < NE:
                            low_hidden(k, e + 1)
                        expert(k, e)
                        if nxt and e == 0:
                            n = x1(nxt)
                        if nxt and e == 1:
                            n = norm_stats(nxt, n)
                        if nxt and e == 2:
                            n = tokens(nxt, n)
                        if nxt and e == 4:
                            low_tokens(nxt)
                            n = choose(nxt, n)
                        if nxt and e == 5:
                            n = combine(nxt, n)
                        if nxt and e == 7:
                            add_bias(nxt, n)

                dve.wait_ge(f["iota"], 1)
                k = chunk_of(0, 0)
                n = x1(k)
                n = tokens(k, norm_stats(k, n))
                low_tokens(k)
                n = combine(k, choose(k, n))
                add_bias(k, n)
                with_next(dve, body)

            @block.tensor
            def _(pe):
                def turn(k):
                    pe.wait_ge(f["relu"], k.c + 1)
                    pe.wait_ge(f["acc_ready"], CREDIT + k.c)
                    for t in range(k.tiles):
                        for kc in range(KC):
                            last = pe.transpose(ps[0:k.rows, t // 2, (t % 2) * C + kc * P:(t % 2) * C + (kc + 1) * P],
                                                gnnT[:, kc, t * P:t * P + k.rows], ident[:, :])
                    last.then_inc(f["turned"], 1)

                def turn_tokens(k):
                    pe.wait_ge(f["normed"], k.c + 1)
                    for t in range(k.tiles):
                        for kc in range(KC):
                            last = pe.transpose(ps[:, kc, t * P:t * P + k.rows], tok[0:k.rows, t, kc * P:(kc + 1) * P],
                                                ident[0:k.rows, 0:k.rows])
                    last.then_inc(f["tok_turned"], 1)

                def route(k):
                    pe.wait_ge(f["tok_copied"], k.c + 1)
                    for t in range(k.tiles):
                        for kc in range(KC):
                            last = pe.matmul(ps[0:k.rows, 2, t * NE:(t + 1) * NE], tokT[:, kc, t * P:t * P + k.rows],
                                             v_rw[:, kc, :], start=(kc == 0), stop=(kc == KC - 1), skip_group_check=True)
                    last.then_inc(f["routed"], 1)

                def turn_comb(k):
                    pe.wait_ge(f["combined"], k.c + 1)
                    for t in range(k.tiles):
                        last = pe.transpose(ps[0:NE, 2, t * P:t * P + k.rows], comb[k.u][0:k.rows, t, :],
                                            ident[0:k.rows, 0:k.rows])
                    last.then_inc(f["comb_turned"], 1)

                def bias(k):
                    pe.wait_ge(f["comb_copied"], k.c + 1)
                    for t in range(k.tiles):
                        last = pe.matmul(ps[0:k.rows, t // 2, (t % 2) * C:(t % 2 + 1) * C], combT[:, t * P:t * P + k.rows],
                                         eb2, start=True, stop=True)
                    last.then_inc(f["b2_done"], 1)

                def layer1(k, e):
                    if e == 0:
                        pe.wait_ge(f["tok_lo"], k.c + 1)
                    pe.wait_ge(f["w_split"], 2 * e + 2)
                    for mt in range(KC):
                        if e > 0:
                            pe.wait_ge(f["hidden"], 2 * NE * k.c + 2 * (e - 1) + mt + 1)
                        m = slice(mt * P, (mt + 1) * P)
                        terms = [(w[:, e, kc, m], x[:, kc, 0:k.n]) for kc in range(KC)
                                 for w, x in products(ew1_hi, ew1_lo, tok_hi[k.u], tok_lo[k.u])]
                        for n, (w, x) in enumerate(terms):
                            last = pe.matmul(ps[:, 3 + mt, 0:k.n], w, x, start=(n == 0), stop=(n == len(terms) - 1))
                        last.then_inc(f["l1"], 1)

                def layer2(k, e):
                    pe.wait_ge(f["hidden"], 2 * NE * k.c + 2 * e + 2)
                    pe.wait_ge(f["hid_lo"], 2 * NE * k.c + 2 * e + 2)
                    pe.wait_ge(f["added"], CREDIT + NE * k.c + e)
                    for t in range(k.tiles):
                        terms = [(h[:, kc, t * P:t * P + k.rows], w[:, e, kc, :]) for kc in range(KC)
                                 for h, w in products(hid_hi[e % 2], hid_lo[e % 2], ew2_hi, ew2_lo)]
                        for n, (h, w) in enumerate(terms):
                            last = pe.matmul(ps[0:k.rows, 5 + t // 2, (t % 2) * C:(t % 2 + 1) * C], h, w,
                                             start=(n == 0), stop=(n == len(terms) - 1), skip_group_check=True)
                    last.then_inc(f["l2"], 1)

                def body(k, nxt):
                    for e in range(NE):
                        if e + 1 < NE:
                            layer1(k, e + 1)
                        if nxt and e == 0:
                            turn(nxt)
                        if nxt and e == 7:
                            turn_comb(nxt)
                        layer2(k, e)
                        if nxt and e == 3:
                            turn_tokens(nxt)
                        if nxt and e == 4:
                            route(nxt)
                    if nxt:
                        layer1(nxt, 0)
                        bias(nxt)

                for credited in (f["turned"], f["l2"], f["tok_turned"], f["added"], f["acc_ready"], f["stored0"], f["stored1"]):
                    pe.sem_inc(credited, CREDIT)
                k = chunk_of(0, 0)
                turn(k), turn_tokens(k), route(k), layer1(k, 0), turn_comb(k), bias(k)
                with_next(pe, body)


_INS = ['x', 'src', 'dst', 'edge_attr_256', 'L0_gnn_W1', 'L0_gnn_b1', 'L0_gnn_bn_gamma', 'L0_gnn_bn_beta', 'L0_gnn_W2',
        'L0_gnn_b2', 'L0_gnn_ln_w', 'L0_gnn_ln_b', 'L0_gnn_gn_w', 'L0_gnn_gn_b', 'L0_gnn_gn_ms', 'L0_mix_wq', 'L0_mix_wk',
        'L0_mix_wv', 'L0_mix_wo', 'L0_mix_bo', 'L0_mix_ln_k_g', 'L0_mix_ln_k_b', 'L0_mix_ln_v_g', 'L0_mix_ln_v_b',
        'L0_ffn_router_w', 'L0_ffn_w1', 'L0_ffn_b1', 'L0_ffn_w2', 'L0_ffn_b2']


def program(nc, a, out):
    def group(prefix):
        return {n[len(prefix):]: v for n, v in a.items() if n.startswith(prefix)}
    build(nc, a["x"], a["src"], a["dst"], a["edge_attr_256"], group("L0_gnn_"), group("L0_mix_"), group("L0_ffn_"), out)


def kernel(**inputs):
    import numpy as _np
    import concourse.bacc as _bacc
    from concourse import mybir as _mybir
    from concourse.bass_utils import run_bass_kernel_spmd as _run

    nc = _bacc.Bacc("TRN2", target_bir_lowering=False, num_devices=1)
    arrays, args = {}, {}
    for name in _INS:
        a = _np.ascontiguousarray(inputs[name])
        arrays[f"in_{name}_dram"] = a
        args[name] = nc.dram_tensor(f"in_{name}_dram", a.shape, _mybir.dt.from_np(a.dtype), kind="ExternalInput").ap()
    out = nc.dram_tensor("out_0_dram", args["x"].shape, _mybir.dt.float32, kind="ExternalOutput").ap()
    program(nc, args, out)
    r = _run(nc, [arrays], core_ids=[0])
    return r.results[0]["out_0_dram"]
```
